# Optimizing a Trainium2 kernel written in Bass

```python
import numpy as np
import jax
import jax.numpy as jnp

def _softmax(x, axis=-1):
    return jax.nn.softmax(x, axis=axis)

def _gelu(x):
    return jax.nn.gelu(x, approximate=True)

def _silu(x):
    return jax.nn.silu(x)

def _sigmoid(x):
    return jax.nn.sigmoid(x)

def _layernorm(x, axis=-1, eps=1e-05):
    m = jnp.mean(x, axis=axis, keepdims=True)
    v = jnp.var(x, axis=axis, keepdims=True)
    return (x - m) / jnp.sqrt(v + eps)

def _scatter_add(tgt, idx, src, axis=0):
    return tgt.at[idx].add(src)

def _segment_sum(src, seg, n):
    return jax.ops.segment_sum(src, seg, n)
kernel_name = 'mk_xattn_seq_d2_seqx_r8_9fc186'

def setup_inputs(seed: int=0):
    np.random.seed(seed)
    _w = jnp.asarray

    def _rec_inputs():
        import jax
        import jax.numpy as jnp
        _rk = jax.random.key(seed)
        x = -0.0002928 + 1 * jax.random.normal(jax.random.fold_in(_rk, 1), (64, 128, 128), jnp.float32)
        _lenS = 128 - jax.random.randint(jax.random.fold_in(_rk, 7), (64,), 0, max(1, 128 // 4) + 1, jnp.int32)
        _lenS2 = 77 - jax.random.randint(jax.random.fold_in(_rk, 8), (64,), 0, max(1, 77 // 4) + 1, jnp.int32)
        _ctx_768P = jax.random.normal(jax.random.fold_in(_rk, 11), (64, 16, 96), jnp.float32)
        _ctx_768c = jax.random.dirichlet(jax.random.fold_in(_rk, 511), 0.3 * jnp.ones((16,), jnp.float32), (64, 77))
        _ctx_768t = jnp.einsum('bsk,bkd->bsd', _ctx_768c, _ctx_768P)
        _ctx_768t = _ctx_768t * jax.lax.rsqrt(jnp.mean(jnp.square(_ctx_768t)) + 1e-12) * 0.953939
        ctx_768 = -0.00423632 + 0.9977 * (_ctx_768t + 0.3 * jax.random.normal(jax.random.fold_in(_rk, 611), (64, 77, 96), jnp.float32))
        return (x, ctx_768)
    x, ctx_768 = _rec_inputs()

    def _L0_xattn_setup():
        import jax, jax.numpy as jnp
        import numpy as np
        D = 128
        H = 16
        DH = 64
        I = H * DH
        DC = 96
        FF = 4 * D
        EPS = 1e-05
        SCALE = DH ** (-0.5)

        def layer_norm(x, g, b):
            m = jnp.mean(x, axis=-1, keepdims=True)
            v = jnp.mean(jnp.square(x - m), axis=-1, keepdims=True)
            return (x - m) * jax.lax.rsqrt(v + EPS) * g + b

        def cross_attention(x, ctx, Wq, Wk, Wv, Wo, bo):
            B, N, _ = x.shape
            M = ctx.shape[1]
            q = (x @ Wq).reshape(B, N, H, DH).transpose(0, 2, 1, 3)
            k = (ctx @ Wk).reshape(B, M, H, DH).transpose(0, 2, 1, 3)
            v = (ctx @ Wv).reshape(B, M, H, DH).transpose(0, 2, 1, 3)
            sim = jnp.einsum('bhid,bhjd->bhij', q, k) * SCALE
            attn = jax.nn.softmax(sim, axis=-1)
            out = jnp.einsum('bhij,bhjd->bhid', attn, v)
            out = out.transpose(0, 2, 1, 3).reshape(B, N, I)
            return out @ Wo + bo
        key = jax.random.key(seed)
        ks = jax.random.split(key, 20)
        s = 0.02
        inp = {'x': jax.random.normal(ks[0], (2, 256, D), jnp.float32), 'context': jax.random.normal(ks[1], (2, 77, DC), jnp.float32), 'ln1_g': jnp.ones((D,), jnp.float32), 'ln1_b': jnp.zeros((D,), jnp.float32), 'ln2_g': jnp.ones((D,), jnp.float32), 'ln2_b': jnp.zeros((D,), jnp.float32), 'ln3_g': jnp.ones((D,), jnp.float32), 'ln3_b': jnp.zeros((D,), jnp.float32), 'Wq1': jax.random.normal(ks[2], (D, I), jnp.float32) * s, 'Wk1': jax.random.normal(ks[3], (D, I), jnp.float32) * s, 'Wv1': jax.random.normal(ks[4], (D, I), jnp.float32) * s, 'Wo1': jax.random.normal(ks[5], (I, D), jnp.float32) * s, 'bo1': jnp.zeros((D,), jnp.float32), 'Wq2': jax.random.normal(ks[6], (D, I), jnp.float32) * s, 'Wk2': jax.random.normal(ks[7], (DC, I), jnp.float32) * s, 'Wv2': jax.random.normal(ks[8], (DC, I), jnp.float32) * s, 'Wo2': jax.random.normal(ks[9], (I, D), jnp.float32) * s, 'bo2': jnp.zeros((D,), jnp.float32), 'Wff1': jax.random.normal(ks[10], (D, 2 * FF), jnp.float32) * s, 'bff1': jnp.zeros((2 * FF,), jnp.float32), 'Wff2': jax.random.normal(ks[11], (FF, D), jnp.float32) * s, 'bff2': jnp.zeros((D,), jnp.float32)}
        return inp
    _L0_xattn_all = _L0_xattn_setup()
    _L0_xattn_in = {k: v for k, v in _L0_xattn_all.items() if k in ('ln1_g', 'ln1_b', 'ln2_g', 'ln2_b', 'ln3_g', 'ln3_b', 'Wq1', 'Wk1', 'Wv1', 'Wo1', 'bo1', 'Wq2', 'Wk2', 'Wv2', 'Wo2', 'bo2', 'Wff1', 'bff1', 'Wff2', 'bff2')}
    del _L0_xattn_all

    def _L1_xattn_setup():
        import jax, jax.numpy as jnp
        import numpy as np
        HEADS = 16
        D_HEAD = 64
        EPS = 1e-05

        def _ln(x, g, b):
            m = jnp.mean(x, axis=-1, keepdims=True)
            v = jnp.var(x, axis=-1, keepdims=True)
            return (x - m) * jax.lax.rsqrt(v + EPS) * g + b

        def _attn(xq, xc, Wq, Wk, Wv, Wo, bo):
            B, N, _ = xq.shape
            S = xc.shape[1]
            q = (xq @ Wq).reshape(B, N, HEADS, D_HEAD)
            k = (xc @ Wk).reshape(B, S, HEADS, D_HEAD)
            v = (xc @ Wv).reshape(B, S, HEADS, D_HEAD)
            scale = D_HEAD ** (-0.5)
            scores = jnp.einsum('bnhd,bshd->bhns', q, k) * scale
            attn = jax.nn.softmax(scores, axis=-1)
            out = jnp.einsum('bhns,bshd->bnhd', attn, v).reshape(B, N, HEADS * D_HEAD)
            return out @ Wo + bo

        def _geglu_ff(x, Wp, bp, Wf, bf):
            h = x @ Wp + bp
            a, gate = jnp.split(h, 2, axis=-1)
            return a * jax.nn.gelu(gate, approximate=False) @ Wf + bf
        key = jax.random.key(seed)
        ks = jax.random.split(key, 16)
        dim, ctx, inner, ffin = (128, 96, HEADS * D_HEAD, 4 * 128)

        def w(k, i, o):
            return jax.random.normal(k, (i, o), jnp.float32) * i ** (-0.5)
        inp = {'x': jax.random.normal(ks[0], (4, 256, dim), jnp.float32), 'context': jax.random.normal(ks[1], (4, 77, ctx), jnp.float32), 'Wq1': w(ks[2], dim, inner), 'Wk1': w(ks[3], dim, inner), 'Wv1': w(ks[4], dim, inner), 'Wo1': w(ks[5], inner, dim), 'bo1': jnp.zeros((dim,), jnp.float32), 'Wq2': w(ks[6], dim, inner), 'Wk2': w(ks[7], ctx, inner), 'Wv2': w(ks[8], ctx, inner), 'Wo2': w(ks[9], inner, dim), 'bo2': jnp.zeros((dim,), jnp.float32), 'Wp': w(ks[10], dim, 2 * ffin), 'bp': jnp.zeros((2 * ffin,), jnp.float32), 'Wf': w(ks[11], ffin, dim), 'bf': jnp.zeros((dim,), jnp.float32), 'g1': jnp.ones((dim,), jnp.float32), 'b1': jnp.zeros((dim,), jnp.float32), 'g2': jnp.ones((dim,), jnp.float32), 'b2': jnp.zeros((dim,), jnp.float32), 'g3': jnp.ones((dim,), jnp.float32), 'b3': jnp.zeros((dim,), jnp.float32)}
        return inp
    _L1_xattn_all = _L1_xattn_setup()
    _L1_xattn_in = {k: v for k, v in _L1_xattn_all.items() if k in ('Wq1', 'Wk1', 'Wv1', 'Wo1', 'bo1', 'Wq2', 'Wk2', 'Wv2', 'Wo2', 'bo2', 'Wp', 'bp', 'Wf', 'bf', 'g1', 'b1', 'g2', 'b2', 'g3', 'b3')}
    del _L1_xattn_all
    return {'x': x, 'ctx_768': ctx_768, 'L0_xattn_ln1_g': _L0_xattn_in['ln1_g'], 'L0_xattn_ln1_b': _L0_xattn_in['ln1_b'], 'L0_xattn_ln2_g': _L0_xattn_in['ln2_g'], 'L0_xattn_ln2_b': _L0_xattn_in['ln2_b'], 'L0_xattn_ln3_g': _L0_xattn_in['ln3_g'], 'L0_xattn_ln3_b': _L0_xattn_in['ln3_b'], 'L0_xattn_Wq1': _L0_xattn_in['Wq1'], 'L0_xattn_Wk1': _L0_xattn_in['Wk1'], 'L0_xattn_Wv1': _L0_xattn_in['Wv1'], 'L0_xattn_Wo1': _L0_xattn_in['Wo1'], 'L0_xattn_bo1': _L0_xattn_in['bo1'], 'L0_xattn_Wq2': _L0_xattn_in['Wq2'], 'L0_xattn_Wk2': _L0_xattn_in['Wk2'], 'L0_xattn_Wv2': _L0_xattn_in['Wv2'], 'L0_xattn_Wo2': _L0_xattn_in['Wo2'], 'L0_xattn_bo2': _L0_xattn_in['bo2'], 'L0_xattn_Wff1': _L0_xattn_in['Wff1'], 'L0_xattn_bff1': _L0_xattn_in['bff1'], 'L0_xattn_Wff2': _L0_xattn_in['Wff2'], 'L0_xattn_bff2': _L0_xattn_in['bff2'], 'L1_xattn_Wq1': _L1_xattn_in['Wq1'], 'L1_xattn_Wk1': _L1_xattn_in['Wk1'], 'L1_xattn_Wv1': _L1_xattn_in['Wv1'], 'L1_xattn_Wo1': _L1_xattn_in['Wo1'], 'L1_xattn_bo1': _L1_xattn_in['bo1'], 'L1_xattn_Wq2': _L1_xattn_in['Wq2'], 'L1_xattn_Wk2': _L1_xattn_in['Wk2'], 'L1_xattn_Wv2': _L1_xattn_in['Wv2'], 'L1_xattn_Wo2': _L1_xattn_in['Wo2'], 'L1_xattn_bo2': _L1_xattn_in['bo2'], 'L1_xattn_Wp': _L1_xattn_in['Wp'], 'L1_xattn_bp': _L1_xattn_in['bp'], 'L1_xattn_Wf': _L1_xattn_in['Wf'], 'L1_xattn_bf': _L1_xattn_in['bf'], 'L1_xattn_g1': _L1_xattn_in['g1'], 'L1_xattn_b1': _L1_xattn_in['b1'], 'L1_xattn_g2': _L1_xattn_in['g2'], 'L1_xattn_b2': _L1_xattn_in['b2'], 'L1_xattn_g3': _L1_xattn_in['g3'], 'L1_xattn_b3': _L1_xattn_in['b3']}

def reference(x, ctx_768, L0_xattn_ln1_g, L0_xattn_ln1_b, L0_xattn_ln2_g, L0_xattn_ln2_b, L0_xattn_ln3_g, L0_xattn_ln3_b, L0_xattn_Wq1, L0_xattn_Wk1, L0_xattn_Wv1, L0_xattn_Wo1, L0_xattn_bo1, L0_xattn_Wq2, L0_xattn_Wk2, L0_xattn_Wv2, L0_xattn_Wo2, L0_xattn_bo2, L0_xattn_Wff1, L0_xattn_bff1, L0_xattn_Wff2, L0_xattn_bff2, L1_xattn_Wq1, L1_xattn_Wk1, L1_xattn_Wv1, L1_xattn_Wo1, L1_xattn_bo1, L1_xattn_Wq2, L1_xattn_Wk2, L1_xattn_Wv2, L1_xattn_Wo2, L1_xattn_bo2, L1_xattn_Wp, L1_xattn_bp, L1_xattn_Wf, L1_xattn_bf, L1_xattn_g1, L1_xattn_b1, L1_xattn_g2, L1_xattn_b2, L1_xattn_g3, L1_xattn_b3):
    import jax
    import jax.numpy as jnp

    def _L0_xattn_ref(x, context, ln1_g, ln1_b, ln2_g, ln2_b, ln3_g, ln3_b, Wq1, Wk1, Wv1, Wo1, bo1, Wq2, Wk2, Wv2, Wo2, bo2, Wff1, bff1, Wff2, bff2):
        import jax, jax.numpy as jnp
        import numpy as np
        D = 128
        H = 16
        DH = 64
        I = H * DH
        DC = 96
        FF = 4 * D
        EPS = 1e-05
        SCALE = DH ** (-0.5)

        def layer_norm(x, g, b):
            m = jnp.mean(x, axis=-1, keepdims=True)
            v = jnp.mean(jnp.square(x - m), axis=-1, keepdims=True)
            return (x - m) * jax.lax.rsqrt(v + EPS) * g + b

        def cross_attention(x, ctx, Wq, Wk, Wv, Wo, bo):
            B, N, _ = x.shape
            M = ctx.shape[1]
            q = (x @ Wq).reshape(B, N, H, DH).transpose(0, 2, 1, 3)
            k = (ctx @ Wk).reshape(B, M, H, DH).transpose(0, 2, 1, 3)
            v = (ctx @ Wv).reshape(B, M, H, DH).transpose(0, 2, 1, 3)
            sim = jnp.einsum('bhid,bhjd->bhij', q, k) * SCALE
            attn = jax.nn.softmax(sim, axis=-1)
            out = jnp.einsum('bhij,bhjd->bhid', attn, v)
            out = out.transpose(0, 2, 1, 3).reshape(B, N, I)
            return out @ Wo + bo
        x = cross_attention(layer_norm(x, ln1_g, ln1_b), layer_norm(x, ln1_g, ln1_b), Wq1, Wk1, Wv1, Wo1, bo1) + x
        x = cross_attention(layer_norm(x, ln2_g, ln2_b), context, Wq2, Wk2, Wv2, Wo2, bo2) + x
        hg = layer_norm(x, ln3_g, ln3_b) @ Wff1 + bff1
        h, gate = (hg[..., :FF], hg[..., FF:])
        ff = h * jax.nn.gelu(gate, approximate=False) @ Wff2 + bff2
        return ff + x

    def _L1_xattn_ref(x, context, Wq1, Wk1, Wv1, Wo1, bo1, Wq2, Wk2, Wv2, Wo2, bo2, Wp, bp, Wf, bf, g1, b1, g2, b2, g3, b3):
        import jax, jax.numpy as jnp
        import numpy as np
        HEADS = 16
        D_HEAD = 64
        EPS = 1e-05

        def _ln(x, g, b):
            m = jnp.mean(x, axis=-1, keepdims=True)
            v = jnp.var(x, axis=-1, keepdims=True)
            return (x - m) * jax.lax.rsqrt(v + EPS) * g + b

        def _attn(xq, xc, Wq, Wk, Wv, Wo, bo):
            B, N, _ = xq.shape
            S = xc.shape[1]
            q = (xq @ Wq).reshape(B, N, HEADS, D_HEAD)
            k = (xc @ Wk).reshape(B, S, HEADS, D_HEAD)
            v = (xc @ Wv).reshape(B, S, HEADS, D_HEAD)
            scale = D_HEAD ** (-0.5)
            scores = jnp.einsum('bnhd,bshd->bhns', q, k) * scale
            attn = jax.nn.softmax(scores, axis=-1)
            out = jnp.einsum('bhns,bshd->bnhd', attn, v).reshape(B, N, HEADS * D_HEAD)
            return out @ Wo + bo

        def _geglu_ff(x, Wp, bp, Wf, bf):
            h = x @ Wp + bp
            a, gate = jnp.split(h, 2, axis=-1)
            return a * jax.nn.gelu(gate, approximate=False) @ Wf + bf
        x = _attn(_ln(x, g1, b1), _ln(x, g1, b1), Wq1, Wk1, Wv1, Wo1, bo1) + x
        x = _attn(_ln(x, g2, b2), context, Wq2, Wk2, Wv2, Wo2, bo2) + x
        x = _geglu_ff(_ln(x, g3, b3), Wp, bp, Wf, bf) + x
        return x
    x = _L0_xattn_ref(x, ctx_768, L0_xattn_ln1_g, L0_xattn_ln1_b, L0_xattn_ln2_g, L0_xattn_ln2_b, L0_xattn_ln3_g, L0_xattn_ln3_b, L0_xattn_Wq1, L0_xattn_Wk1, L0_xattn_Wv1, L0_xattn_Wo1, L0_xattn_bo1, L0_xattn_Wq2, L0_xattn_Wk2, L0_xattn_Wv2, L0_xattn_Wo2, L0_xattn_bo2, L0_xattn_Wff1, L0_xattn_bff1, L0_xattn_Wff2, L0_xattn_bff2)
    x = _L1_xattn_ref(x, ctx_768, L1_xattn_Wq1, L1_xattn_Wk1, L1_xattn_Wv1, L1_xattn_Wo1, L1_xattn_bo1, L1_xattn_Wq2, L1_xattn_Wk2, L1_xattn_Wv2, L1_xattn_Wo2, L1_xattn_bo2, L1_xattn_Wp, L1_xattn_bp, L1_xattn_Wf, L1_xattn_bf, L1_xattn_g1, L1_xattn_b1, L1_xattn_g2, L1_xattn_b2, L1_xattn_g3, L1_xattn_b3)
    return x

_drawn_inputs = setup_inputs


def setup_inputs(seed=0):
    import zlib

    import numpy as np

    out = dict(_drawn_inputs(seed))
    spreads = {'L0_xattn_ln1_g': (1.0, 0.6),
     'L0_xattn_ln1_b': (0.0, 0.431),
     'L0_xattn_ln2_g': (1.0, 0.6),
     'L0_xattn_ln2_b': (0.0, 0.8),
     'L0_xattn_ln3_g': (1.0, 0.6),
     'L0_xattn_ln3_b': (0.0, 0.8),
     'L0_xattn_bo1': (0.0, 0.1),
     'L0_xattn_bo2': (0.0, 0.1),
     'L0_xattn_bff1': (0.0, 0.8),
     'L0_xattn_bff2': (0.0, 0.1),
     'L1_xattn_bo1': (0.0, 0.1),
     'L1_xattn_bo2': (0.0, 0.275),
     'L1_xattn_bp': (0.0, 0.269),
     'L1_xattn_bf': (0.0, 0.279),
     'L1_xattn_g1': (1.0, 0.549),
     'L1_xattn_b1': (0.0, 0.1),
     'L1_xattn_g2': (1.0, 0.6),
     'L1_xattn_b2': (0.0, 0.975),
     'L1_xattn_g3': (1.0, 0.2),
     'L1_xattn_b3': (0.0, 0.1)}
    factors = {'L0_xattn_Wq1': 8.0,
     'L0_xattn_Wk1': 8.0,
     'L0_xattn_Wq2': 8.0,
     'L0_xattn_Wk2': 8.0,
     'L0_xattn_Wff1': 3.5,
     'L0_xattn_Wff2': 3.366}
    for name, (base, spread) in spreads.items():
        noise = np.random.default_rng([zlib.crc32(name.encode()), seed]).standard_normal(out[name].shape)
        drawn = base * np.exp(spread * noise) if base else spread * noise
        out[name] = jnp.asarray(drawn.astype(out[name].dtype))
    for name, factor in factors.items():
        out[name] = (out[name] * factor).astype(out[name].dtype)
    return out
```

```python
from contextlib import ExitStack

import concourse.bass as bass
from concourse import mybir

F32 = mybir.dt.float32
F32R = mybir.dt.float32r
ALU = mybir.AluOpType
ACT = mybir.ActivationFunctionType
AX = mybir.AxisListType

P = 128
HEADS, DH = 16, 64
INNER = HEADS * DH
CHUNKS = INNER // P
HG = 4
UPB = HEADS // HG
LAYERS = 2
EPS = 1e-5
PS_BANK = 512
VRING = 4
PRING = 4
T_LAG, PV_LAG, Y_LAG = 2, 3, 4


class Attention:

    def __init__(self, name, batches, group, keys, kv_dim, heads_per_item):
        self.name, self.B, self.G, self.J, self.E = name, batches, group, keys, kv_dim
        self.JP = keys + keys % 2
        self.GJ = group * self.JP
        self.HI = heads_per_item
        self.U = UPB * group
        self.UB = 2 * self.U
        self.NI = batches // (2 * group)
        self.groups = batches // group
        self.units = UPB * batches
        self.w_per_group = HEADS // heads_per_item
        self.plan = []
        rest = list(range(self.w_per_group))
        for s in range(self.U):
            here = []
            if s >= 2:
                steps_left = self.U - s
                n = 1 if len(rest) <= steps_left or s % 4 >= 2 and len(rest) <= steps_left + 2 else 2
                here += [("w", rest.pop(0)) for _ in range(min(n, len(rest)))]
            if s % 4 >= 2:
                here.append(("v", s // 4, s % 4 - 2))
            self.plan.append(here)
        assert not rest
        self.v_ahead = 2
        self.items_per_body = 2 * (self.w_per_group + 2 * group)
        self.items_prologue = self.w_per_group + 2 * self.v_ahead
        self.items = self.w_per_group * self.groups + 2 * batches

    def body(self, last):
        out, n, w, v = [[] for _ in range(self.UB)], 0, 0, 0
        for s in range(self.UB):
            for it in self.plan[s % self.U]:
                if it[0] == "w":
                    if last and s >= self.U:
                        continue
                    out[s].append(("w", it[1], 1 - s // self.U, n, w))
                    w += 1
                else:
                    b = s // UPB + self.v_ahead
                    if last and b >= 2 * self.G:
                        continue
                    out[s].append(("v", b, it[2], n, v))
                    v += 1
                n += 1
        return out

    def v_count(self, i, b, first, last):
        if b < self.v_ahead:
            if first:
                return self.w_per_group + 2 * b + 2
            plan, off = self.body(False), b + 2 * self.G
            n = next(it[3] for s in plan for it in s if it[:3] == ("v", off, 1)) - self.items_per_body
        else:
            n = next(it[3] for s in self.body(last) for it in s if it[:3] == ("v", b, 1))
        return i * self.items_per_body + (self.items_prologue + n + 1)

    def prologue(self):
        out = [("w", j, 0, j, j) for j in range(self.w_per_group)]
        for b in range(self.v_ahead):
            for half in range(2):
                v = 2 * b + half
                out.append(("v", b, half, self.w_per_group + v, v))
        return out


def block_kernel(nc, x_in, ctx_t, wq_t, wk_t, wv, wo, bo, wk2_t, wv2, ln_g, ln_b, w1, b1, w2, out):
    B = x_in.shape[0]
    J2 = ctx_t.shape[2]
    E2 = ctx_t.shape[0]
    FF = w1.shape[2] // 2
    FC = FF // P
    FG = 4
    FN = FG * P
    FNI = B // (2 * FG)
    SELF = Attention("self", B, 2, P, P, 2)
    CROSS = Attention("ctx", B, 4, J2, E2, 1)
    PHASES = (SELF, CROSS)
    GMAX = 4

    ctx = ExitStack()
    with ctx:
        def sb(name, shape, dt=F32):
            return ctx.enter_context(nc.sbuf_tensor(name, shape, dt))

        def sem(name):
            return ctx.enter_context(nc.semaphore(name))

        x = sb("x", [P, B, P])
        stats = sb("stats", [P, B, 6])
        lnst = sb("lnst", [P, 6, B])
        rstd = sb("rstd", [P, B])
        nmr = sb("nmr", [P, B])
        ident = sb("ident", [P, P])
        xn = sb("xn", [P, GMAX, P])
        xfull = sb("xfull", [P, GMAX * P])
        xt_hi = sb("xt_hi", [P, 2, GMAX * P], F32R)
        xt_lo = sb("xt_lo", [P, 2, GMAX * P], F32R)
        craw = sb("craw", [E2, GMAX, J2 + J2 % 2])
        c_hi = sb("c_hi", [E2, 2, CROSS.GJ], F32R)
        c_lo = sb("c_lo", [E2, 2, CROSS.GJ], F32R)
        a_hi = sb("a_hi", [P, HEADS, P], F32R)
        a_lo = sb("a_lo", [P, HEADS, P], F32R)
        wv_hi = sb("wv_hi", [P, INNER], F32R)
        wv_lo = sb("wv_lo", [P, INNER], F32R)
        wo_sb = sb("wo_sb", [P, CHUNKS, P])
        bo_bc = sb("bo_bc", [P, P])
        gb = sb("gb", [P, 2])
        w_hi = sb("w_hi", [P, 2, HEADS * CROSS.GJ], F32R)
        w_lo = sb("w_lo", [P, 2, HEADS * CROSS.GJ], F32R)
        v_sb = sb("v_sb", [P, VRING, INNER])
        probs = sb("probs", [P, PRING, HG, P])
        nmax = sb("nmax", [P, PRING, HG])
        rsum = sb("rsum", [P, PRING, HG])
        rrec = sb("rrec", [P, PRING, HG])
        pt = sb("pt", [P, 2, HG * P])
        ot = sb("ot", [P, 2, CHUNKS, P])
        ytmp = sb("ytmp", [P, P])
        fb = sb("fb", [P, 2 * FC])
        raw = v_sb
        raw_q, raw_k = raw[:, 0, :], raw[:, 1, :]
        raw_v = raw[:, 2, :]
        f1_hi = a_hi[:, 0:2 * FC, :].rearrange("p c n -> p (c n)")
        f1_lo = a_lo[:, 0:2 * FC, :].rearrange("p c n -> p (c n)")
        f2_sb = wo_sb[:, 0:FC, :]
        gel = probs[:].rearrange("p a b c -> p a (b c)")
        raw_f = ot[:, 0, :, :].rearrange("p c n -> p (c n)")
        hid = v_sb[:].rearrange("p (a b) (c n) -> p a (b c) n", a=2, n=FN)

        def bank(name):
            return ctx.enter_context(nc.psum_tensor(name, [P, PS_BANK], F32))
        sc_ps = [bank(f"sc_ps{i}") for i in range(2)]
        tr_ps = [bank(f"tr_ps{i}") for i in range(2)]
        it_ps = [bank(f"it_ps{i}") for i in range(2)]
        ot_ps = bank("ot_ps")
        y_ps = bank("y_ps")

        x_loaded = [sem(f"x_loaded{i}") for i in range(4)]
        x_stats0 = sem("x_stats0")
        ident_zero, ident_ready, pad_ready = sem("ident_zero"), sem("ident_ready"), sem("pad_ready")
        chain = sem("chain")
        var_ready, std_ready = sem("var_ready"), sem("std_ready")
        phase_open = sem("phase_open")
        raw_in = sem("raw_in")
        wprod_ps, wprod_hi, wprod_lo = sem("wprod_ps"), sem("wprod_hi"), sem("wprod_lo")
        wv_hi_s, wv_lo_s = sem("wv_hi_s"), sem("wv_lo_s")
        f1_hi_s, f1_lo_s = sem("f1_hi_s"), sem("f1_lo_s")
        out_done = sem("out_done")
        S = {}
        for ph in PHASES:
            S[ph.name] = {k: sem(f"{ph.name}_{k}") for k in (
                "scores", "nmax", "exps", "recips", "normed", "turned", "pt", "pv", "ot", "y", "ysum",
                "resid", "item", "whi", "evac", "xn", "xnT", "xhi", "xfull", "xlo", "craw", "chi", "clo")}
        FS = {k: sem(f"ff_{k}") for k in ("xn", "xnT", "xhi", "xfull", "xlo", "gate", "a", "gelu", "hid",
                                          "y", "ysum", "resid")}

        CHAIN = 10
        CHAIN_LAYER = 3 * CHAIN
        RAW_DMAS = (6, 6, 4)
        RAW_BEFORE = (0, 6, 12)
        RAW_LAYER = 16

        def open_phase(eng, L, n):
            eng.wait_ge(phase_open, L * 3 + (n + 1))

        def batch_of(i, ph_or_g, b):
            return i * (2 * ph_or_g) + b

        block = ctx.enter_context(nc.Block())

        def bodies(eng, NI, steps, lag, step):
            for s in range(steps):
                step(0, s, True, False)
            with eng.Fori(1, NI - 1) as i:
                for s in range(steps):
                    step(i, s, False, False)
            for s in range(steps + lag):
                step(NI - 1, s, False, True)

        def exists(ph_steps, s, first, last, lag):
            return not (first and s < lag) and not (last and s - lag >= ph_steps)

        @block.sync
        def _(sp):
            q = B // 4
            for c in range(4):
                sp.dma_start(x[:, c * q:(c + 1) * q, :],
                             x_in[c * q:(c + 1) * q].rearrange("b t d -> t b d")).then_inc(x_loaded[c], 16)
            for L in range(LAYERS):
                for n, ph in enumerate(PHASES):
                    c = S[ph.name]
                    sp.wait_ge(phase_open, L * 3 + (n + 1))
                    kt, vv = (wk_t, wv) if n == 0 else (wk2_t, wv2)
                    E = ph.E
                    sp.dma_start(raw_q.rearrange("p (c n) -> p c n", c=CHUNKS),
                                 wq_t[L, n].rearrange("(c p) n -> p c n", p=P)).then_inc(raw_in, 16)
                    sp.dma_start(raw_k[:, 0:CHUNKS * E].rearrange("p (c n) -> p c n", c=CHUNKS),
                                 kt[L].rearrange("(c p) n -> p c n", p=P)).then_inc(raw_in, 16)
                    sp.dma_start(raw_v[0:E, :], vv[L]).then_inc(raw_in, 16)
                    sp.dma_start(wo_sb[:], wo[L, n].rearrange("(c p) n -> p c n", p=P)).then_inc(raw_in, 16)
                    sp.dma_start(bo_bc[:], bo[L, n:n + 1, :].to_broadcast([P, P])).then_inc(raw_in, 16)
                    sp.dma_start(gb[:], ln_g[L, n]).then_inc(raw_in, 16)
                    if n == 1:
                        sp.wait_ge(pad_ready, 1)
                        sp.dma_start(craw[:, :, 0:J2], ctx_t[:, 0:ph.G, :]).then_inc(c["craw"], 16)
                        with sp.Fori(1, ph.groups) as g:
                            sp.wait_ge(c["clo"], L * ph.groups + g)
                            sp.dma_start(craw[:, :, 0:J2], ctx_t[:, bass.ts(g, ph.G), :]).then_inc(c["craw"], 16)
                sp.wait_ge(phase_open, L * 3 + 3)
                sp.dma_start(raw_f, w1[L]).then_inc(raw_in, 16)
                sp.dma_start(f2_sb, w2[L].rearrange("(c p) n -> p c n", p=P)).then_inc(raw_in, 16)
                sp.dma_start(bo_bc[:], bo[L, 2:3, :].to_broadcast([P, P])).then_inc(raw_in, 16)
                sp.dma_start(gb[:], ln_g[L, 2]).then_inc(raw_in, 16)
                sp.dma_start(fb[:], b1[L]).then_inc(raw_in, 16)
            sp.wait_ge(FS["resid"], LAYERS * B)
            for c in range(4):
                sp.dma_start(out[c * q:(c + 1) * q].rearrange("b t d -> t b d"),
                             x[:, c * q:(c + 1) * q, :]).then_inc(out_done, 16)
            sp.wait_ge(out_done, 64)

        RAW_DMAS_N = (6, 6, 5)

        def raw_ready(eng, L, n):
            eng.wait_ge(raw_in, L * (16 * sum(RAW_DMAS_N)) + 16 * sum(RAW_DMAS_N[:n + 1]))

        @block.gpsimd
        def _(pool):
            nc.gpsimd.memset(ident[:], 0.0).then_inc(ident_zero, 1)
            nc.gpsimd.memset(craw[:], 0.0).then_inc(pad_ready, 1)
            pool.wait_ge(ident_zero, 1)
            nc.gpsimd.affine_select(out=ident[:], in_=ident[:], compare_op=ALU.not_equal, fill=1.0,
                                    base=0, pattern=[[-1, P]], channel_multiplier=1).then_inc(ident_ready, 1)

            def phase(ph, L):
                c = S[ph.name]
                base = L * ph.units

                def step(i, s, first, last):
                    if not exists(ph.UB, s, first, last, 0):
                        return
                    k = base + (i * ph.UB + s)
                    pr = probs[:, s % PRING, :, 0:ph.J]
                    pool.wait_ge(c["recips"], k + 1)
                    nc.gpsimd.tensor_tensor(pr, pr, rrec[:, s % PRING, :].unsqueeze(2).to_broadcast([P, HG, ph.J]),
                                            ALU.mult).then_inc(c["normed"], 1)

                bodies(pool, ph.NI, ph.UB, 0, step)

            for L in range(LAYERS):
                for ph in PHASES:
                    phase(ph, L)

        @block.tensor
        def _(pe):
            def three(out_, l_hi, l_lo, r_hi, r_lo):
                nc.tensor.matmul(out_, l_hi, r_hi, start=True, stop=False)
                nc.tensor.matmul(out_, l_hi, r_lo, start=False, stop=False)
                return nc.tensor.matmul(out_, l_lo, r_hi, start=False, stop=True)

            def turn_rows(c, g_count, G, free_wait):
                pe.wait_ge(c["xn"], g_count)
                for wsem, val in free_wait:
                    pe.wait_ge(wsem, val)
                for b in range(G):
                    last = nc.tensor.transpose(y_ps[:, b * P:(b + 1) * P], xn[:, b, :], ident[:])
                last.then_inc(c["xnT"], 1)

            def attention(n, ph, L):
                c = S[ph.name]
                E, J, JP = ph.E, ph.J, ph.JP
                units, items, groups, batches = L * ph.units, L * ph.items, L * ph.groups, L * ph.B
                open_phase(pe, L, n)
                raw_ready(pe, L, n)
                for r in range(2):
                    for j in range(4):
                        for odd in range(2):
                            h = 8 * r + 2 * j + odd
                            rows = slice(DH * odd, DH * odd + DH)
                            last = nc.tensor.matmul(
                                (sc_ps if r == 0 else tr_ps)[odd][0:E, j * P:(j + 1) * P],
                                raw_k[rows, (h // 2) * E:(h // 2 + 1) * E],
                                raw_q[rows, (h // 2) * P:(h // 2 + 1) * P], start=True, stop=True)
                    last.then_inc(wprod_ps, 1)

                def kv(par, b=None):
                    hi, lo = (xt_hi, xt_lo) if n == 0 else (c_hi, c_lo)
                    if b is None:
                        return hi[0:E, par, 0:ph.GJ], lo[0:E, par, 0:ph.GJ]
                    return hi[0:E, par, b * JP:b * JP + J], lo[0:E, par, b * JP:b * JP + J]

                def item(it, base, first_body):
                    kind, a, z, m, q = it
                    dst = it_ps[m % 2]
                    if not (first_body and m < 2):
                        pe.wait_ge(c["evac"], base + (m - 1))
                    if kind == "w":
                        hi, lo = kv(z)
                        for t in range(ph.HI):
                            h = a * ph.HI + t
                            last = three(dst[:, t * ph.GJ:(t + 1) * ph.GJ], a_hi[0:E, h, :], a_lo[0:E, h, :], hi, lo)
                    else:
                        hi, lo = kv((a // ph.G) % 2, a % ph.G)
                        cols = slice(z * PS_BANK, (z + 1) * PS_BANK)
                        last = three(dst[0:J, :], hi, lo, wv_hi[0:E, cols], wv_lo[0:E, cols])
                    last.then_inc(c["item"], 1)

                def kv_ready(g):
                    pe.wait_ge(c["xlo"], groups + g)
                    if n == 1:
                        pe.wait_ge(c["clo"], groups + g)

                turn_rows(c, groups + 1, ph.G, ())
                pe.wait_ge(wprod_lo, L * 8 + (4 * n + 4))
                pe.wait_ge(wv_lo_s, L * 2 + (n + 1))
                kv_ready(1)
                for it in ph.prologue():
                    item(it, items, True)
                plans = {False: ph.body(False), True: ph.body(True)}

                def step(i, s, first, last_body):
                    k = units + (i * ph.UB + s)
                    if exists(ph.UB, s, first, last_body, 0):
                        g, gs, b = s // ph.U, s % ph.U, s // UPB
                        if gs == 0:
                            pe.wait_ge(c["evac"], items + (i * ph.items_per_body + ph.items_prologue
                                                           + g * (ph.items_per_body // 2)))
                        if not (first and s < 2):
                            pe.wait_ge(c["exps"], k - 1)
                        bank_ = sc_ps[s % 2][:, 0:HG * JP]
                        h0 = HG * (s % UPB)
                        bg = b % ph.G
                        rows = slice(bg * P, (bg + 1) * P)

                        def w(t):
                            return t[:, g % 2, 0:HEADS * ph.GJ].rearrange("p (h j) -> p h j", h=HEADS)[
                                :, h0:h0 + HG, bg * JP:(bg + 1) * JP]
                        three(bank_, xt_hi[:, g % 2, rows], xt_lo[:, g % 2, rows], w(w_hi), w(w_lo)).then_inc(c["scores"], 1)
                        if gs == 1 and not (last_body and g == 1):
                            gn = i * 2 + g
                            bd = i * (2 * ph.G) + g * ph.G
                            fw = () if first and g == 0 else ((c["resid"], batches + (bd - 1)),)
                            turn_rows(c, groups + (gn + 2), ph.G, fw)
                        if gs == 2 and not (last_body and g == 1):
                            kv_ready(i * 2 + g + 2)
                        its = plans[last_body][s]
                        ib = items + (i * ph.items_per_body + ph.items_prologue)
                        for it in its[:1]:
                            item(it, ib, False)
                    else:
                        its = []
                    if exists(ph.UB, s, first, last_body, T_LAG):
                        u = s - T_LAG
                        pe.wait_ge(c["normed"], k - T_LAG + 1)
                        if not (first and u < 2):
                            pe.wait_ge(c["pt"], k - T_LAG - 1)
                        for t in range(HG):
                            last = nc.tensor.transpose(tr_ps[u % 2][0:J, t * P:(t + 1) * P],
                                                       probs[:, u % PRING, t, 0:J], ident[:])
                        last.then_inc(c["turned"], 1)
                    for it in its[1:]:
                        item(it, ib, False)
                    if exists(ph.UB, s, first, last_body, PV_LAG):
                        u = s - PV_LAG
                        b = u // UPB
                        pe.wait_ge(c["pt"], k - PV_LAG + 1)
                        if not (first and u < 1):
                            pe.wait_ge(c["ot"], k - PV_LAG)
                        if u % UPB == 0:
                            pe.wait_ge(c["evac"], items + ph.v_count(i, b, first, last_body))
                        h0 = HG * (u % UPB)
                        for t in range(HG):
                            o = ot_ps[DH * (t % 2):DH * (t % 2) + DH, (t // 2) * P:(t // 2 + 1) * P]
                            last = nc.tensor.matmul(o, v_sb[0:J, b % VRING, (h0 + t) * DH:(h0 + t + 1) * DH],
                                                    pt[0:J, u % 2, t * P:(t + 1) * P], start=True, stop=True)
                        last.then_inc(c["pv"], 1)
                    if exists(ph.UB, s, first, last_body, Y_LAG) and (s - Y_LAG) % UPB == UPB - 1:
                        b = (s - Y_LAG) // UPB
                        bb = batches + (i * (2 * ph.G) + b)
                        pe.wait_ge(c["ot"], k - Y_LAG + 1)
                        if not (first and b < 1):
                            pe.wait_ge(c["ysum"], bb)
                        gl = s // ph.U
                        pe.wait_ge(c["xlo"], groups + (i * 2 + (2 if last_body else gl + 2)))
                        for ch in range(CHUNKS):
                            last = nc.tensor.matmul(y_ps[:, 0:P], ot[:, b % 2, ch, :], wo_sb[:, ch, :],
                                                    start=(ch == 0), stop=(ch == CHUNKS - 1))
                        last.then_inc(c["y"], 1)

                bodies(pe, ph.NI, ph.UB, Y_LAG, step)

            def feed_forward(L):
                c = FS
                groups, batches = L * (B // FG), L * B
                open_phase(pe, L, 2)
                raw_ready(pe, L, 2)
                turn_rows(c, groups + 1, FG, ())
                pe.wait_ge(f1_lo_s, L + 1)

                def step(i, s, first, last_body):
                    g = i * 2 + s
                    u = groups * FC + (i * (2 * FC) + s * FC)
                    if exists(2, s, first, last_body, 0):
                        pe.wait_ge(c["xlo"], groups + (g + 1))
                        hi, lo = xt_hi[:, s % 2, :], xt_lo[:, s % 2, :]
                        for ch in range(FC):
                            ga, aa = sc_ps[ch % 2], tr_ps[ch % 2]
                            if not (first and s == 0 and ch < 2):
                                pe.wait_ge(c["gelu"], u + (ch - 1))
                            cols = slice(FF + ch * P, FF + (ch + 1) * P)
                            three(ga[:], f1_hi[:, cols], f1_lo[:, cols], hi, lo).then_inc(c["gate"], 1)
                            if not (first and s == 0 and ch < 2):
                                pe.wait_ge(c["hid"], u + (ch - 1))
                            cols = slice(ch * P, (ch + 1) * P)
                            three(aa[:], f1_hi[:, cols], f1_lo[:, cols], hi, lo).then_inc(c["a"], 1)
                        if not (last_body and s == 1):
                            turn_rows(c, groups + (g + 2), FG, ())
                    if exists(2, s, first, last_body, 1):
                        for b in range(FG):
                            bb = batches + ((g - 1) * FG + b)
                            if b == 0:
                                pe.wait_ge(c["hid"], u)
                            if not (first and s == 1 and b < 2):
                                pe.wait_ge(c["ysum"], bb - 1)
                            for ch in range(FC):
                                last = nc.tensor.matmul(it_ps[b % 2][:, 0:P],
                                                        hid[:, (s - 1) % 2, ch, b * P:(b + 1) * P],
                                                        f2_sb[:, ch, :], start=(ch == 0), stop=(ch == FC - 1))
                            last.then_inc(c["y"], 1)

                bodies(pe, FNI, 2, 1, step)

            pe.wait_ge(ident_ready, 1)
            for L in range(LAYERS):
                for n, ph in enumerate(PHASES):
                    attention(n, ph, L)
                feed_forward(L)

        @block.scalar
        def _(act):
            def std(L, n):
                act.wait_ge(var_ready, L * 3 + (n + 1))
                nc.scalar.activation(lnst[:, 4, :], lnst[:, 3, :], ACT.Sqrt).then_inc(std_ready, 1)

            def rows_hi(c, count, G, par):
                act.wait_ge(c["xnT"], count)
                nc.scalar.activation(xt_hi[:, par, 0:G * P], y_ps[:, 0:G * P], ACT.Identity,
                                     scale=gb[:, 0:1], bias=gb[:, 1:2]).then_inc(c["xhi"], 1)

            def attention(n, ph, L):
                c = S[ph.name]
                E, J, JP = ph.E, ph.J, ph.JP
                units, items, groups = L * ph.units, L * ph.items, L * ph.groups
                std(L, n)
                open_phase(act, L, n)
                raw_ready(act, L, n)
                for r in range(2):
                    act.wait_ge(wprod_ps, L * 4 + (2 * n + r + 1))
                    for odd in range(2):
                        src = (sc_ps if r == 0 else tr_ps)[odd][0:E, :].rearrange("p (h n) -> p h n", h=4)
                        nc.scalar.activation(a_hi[0:E, 8 * r + odd:8 * r + 8:2, :], src, ACT.Copy,
                                             scale=DH ** -0.5).then_inc(wprod_hi, 1)
                nc.scalar.copy(wv_hi[0:E, :], raw_v[0:E, :]).then_inc(wv_hi_s, 1)

                def group_in(g, par):
                    rows_hi(c, groups + g, ph.G, par)
                    if n == 1:
                        act.wait_ge(c["craw"], groups * 16 + g * 16)
                        nc.scalar.copy(c_hi[:, par, :], craw[:].rearrange("p b j -> p (b j)")).then_inc(c["chi"], 1)

                def item_hi(it, base, wbase):
                    kind, a, z, m, q = it
                    if kind == "w":
                        act.wait_ge(c["item"], base + (m + 1))
                        nc.scalar.copy(w_hi[:, z, a * ph.HI * ph.GJ:(a + 1) * ph.HI * ph.GJ],
                                       it_ps[m % 2][:, 0:ph.HI * ph.GJ]).then_inc(c["whi"], 1)

                group_in(1, 0)
                for it in ph.prologue():
                    item_hi(it, items, 0)
                plans = {False: ph.body(False), True: ph.body(True)}

                def step(i, s, first, last_body):
                    k = units + (i * ph.UB + s)
                    its = []
                    if exists(ph.UB, s, first, last_body, 0):
                        g, gs = s // ph.U, s % ph.U
                        ib = items + (i * ph.items_per_body + ph.items_prologue)
                        its = plans[last_body][s]
                        if gs == 1 and not (last_body and g == 1):
                            group_in(i * 2 + g + 2, 1 - g)
                        for it in its[:1]:
                            item_hi(it, ib, 0)
                        act.wait_ge(c["nmax"], k + 1)
                        if not (first and s < PRING):
                            act.wait_ge(c["turned"], k - PRING + 1)
                        for t in range(HG):
                            last = nc.scalar.activation(
                                probs[:, s % PRING, t, 0:J], sc_ps[s % 2][:, t * JP:t * JP + J], ACT.Exp,
                                bias=nmax[:, s % PRING, t:t + 1], scale=1.0,
                                accum_out=rsum[:, s % PRING, t:t + 1])
                        last.then_inc(c["exps"], 1)
                    if exists(ph.UB, s, first, last_body, T_LAG):
                        u = s - T_LAG
                        act.wait_ge(c["turned"], k - T_LAG + 1)
                        if not (first and u < 2):
                            act.wait_ge(c["pv"], k - T_LAG - 1)
                        nc.scalar.copy(pt[0:J, u % 2, :], tr_ps[u % 2][0:J, :]).then_inc(c["pt"], 1)
                    for it in its[1:]:
                        item_hi(it, ib, 0)

                bodies(act, ph.NI, ph.UB, T_LAG, step)

            def feed_forward(L):
                c = FS
                groups = L * (B // FG)
                std(L, 2)
                open_phase(act, L, 2)
                raw_ready(act, L, 2)
                nc.scalar.copy(f1_hi, raw_f).then_inc(f1_hi_s, 1)
                rows_hi(c, groups + 1, FG, 0)

                def step(i, s, first, last_body):
                    if not exists(2, s, first, last_body, 0):
                        return
                    u = groups * FC + (i * (2 * FC) + s * FC)
                    for ch in range(FC):
                        act.wait_ge(c["gate"], u + (ch + 1))
                        if not (first and s == 0):
                            act.wait_ge(c["hid"], u + (ch + 1 - FC))
                        nc.scalar.activation(gel[:, ch, :], sc_ps[ch % 2][:], ACT.Gelu,
                                             bias=fb[:, FC + ch:FC + ch + 1], scale=1.0).then_inc(c["gelu"], 1)
                    if not (last_body and s == 1):
                        rows_hi(c, groups + (i * 2 + s + 2), FG, 1 - s)

                bodies(act, FNI, 2, 0, step)

            for L in range(LAYERS):
                for n, ph in enumerate(PHASES):
                    attention(n, ph, L)
                feed_forward(L)

        @block.vector
        def _(dve):
            for b in range(B):
                if b % (B // 4) == 0:
                    dve.wait_ge(x_loaded[b // (B // 4)], 16)
                last = nc.vector.bn_stats(stats[:, b, :], x[:, b, :])
            last.then_inc(x_stats0, 1)
            dve.wait_ge(x_stats0, 1)

            def statistics(L, n, prev):
                base = L * CHAIN_LAYER + n * CHAIN
                done = [0]

                def link(ins):
                    done[0] += 1
                    ins.then_inc(chain, 1)
                    dve.wait_ge(chain, base + done[0])

                me, qe, mo, qo = (stats[:, :, j] for j in (1, 2, 4, 5))
                total, diff, q, var, sd, t = (lnst[:, j, :] for j in range(6))
                link(nc.vector.tensor_tensor(total, me, mo, ALU.add))
                link(nc.vector.tensor_tensor(diff, me, mo, ALU.subtract))
                link(nc.vector.tensor_tensor(q, qe, qo, ALU.add))
                link(nc.vector.tensor_tensor(diff, diff, diff, ALU.mult))
                link(nc.vector.scalar_tensor_tensor(out=q, in0=diff, scalar=P / 4.0, in1=q, op0=ALU.mult, op1=ALU.add))
                nc.vector.tensor_scalar(var, q, 1.0 / P, EPS, ALU.mult, ALU.add).then_inc(var_ready, 1)
                dve.wait_ge(std_ready, L * 3 + (n + 1))
                link(nc.vector.reciprocal(rstd[:], sd))
                link(nc.vector.tensor_tensor(t, rstd[:], rstd[:], ALU.mult))
                link(nc.vector.tensor_tensor(t, t, var, ALU.mult))
                link(nc.vector.tensor_scalar(t, t, -0.5, 1.5, ALU.mult, ALU.add))
                link(nc.vector.tensor_tensor(rstd[:], rstd[:], t, ALU.mult))
                assert done[0] == CHAIN
                nc.vector.scalar_tensor_tensor(out=nmr[:], in0=total, scalar=-0.5, in1=rstd[:],
                                               op0=ALU.mult, op1=ALU.mult).then_inc(phase_open, 1)
                dve.wait_ge(phase_open, L * 3 + (n + 1))

            def rows_norm(c, count, G, b0):
                for b in range(G):
                    bb = b0 + b
                    if b == 0 and count is not None:
                        dve.wait_ge(c["xnT"], count)
                    ins = nc.vector.tensor_scalar(xn[:, b, :], x[:, bb, :], rstd[:, bass.ds(bb, 1)],
                                                  nmr[:, bass.ds(bb, 1)], ALU.mult, ALU.add)
                ins.then_inc(c["xn"], 1)

            def rows_lo(c, count, G, par):
                dve.wait_ge(c["xnT"], count)
                dve.wait_ge(c["xhi"], count)
                nc.vector.tensor_scalar(xfull[:, 0:G * P], y_ps[:, 0:G * P], gb[:, 0:1], gb[:, 1:2],
                                        ALU.mult, ALU.add).then_inc(c["xfull"], 1)
                dve.wait_ge(c["xfull"], count)
                nc.vector.tensor_tensor(xt_lo[:, par, 0:G * P], xfull[:, 0:G * P],
                                        xt_hi[:, par, 0:G * P].bitcast(F32), ALU.subtract).then_inc(c["xlo"], 1)

            def residual(c, src, bb, b):
                dve.wait_ge(c["y"], bb + 1)
                nc.vector.tensor_tensor(ytmp[:], src, bo_bc[:], ALU.add).then_inc(c["ysum"], 1)
                dve.wait_ge(c["ysum"], bb + 1)
                nc.vector.tensor_tensor(x[:, b, :], x[:, b, :], ytmp[:], ALU.add).then_inc(c["resid"], 1)
                dve.wait_ge(c["resid"], bb + 1)
                nc.vector.bn_stats(stats[:, b, :], x[:, b, :]).then_inc(c["xstat"], 1)

            def attention(n, ph, L):
                c = S[ph.name]
                E, J, JP = ph.E, ph.J, ph.JP
                units, items, groups, batches = L * ph.units, L * ph.items, L * ph.groups, L * ph.B
                statistics(L, n, None)
                raw_ready(dve, L, n)
                rows_norm(c, None, ph.G, 0)
                for r in range(2):
                    for odd in range(2):
                        src = (sc_ps if r == 0 else tr_ps)[odd][0:E, :].rearrange("p (h n) -> p h n", h=4)
                        heads = slice(8 * r + odd, 8 * r + 8, 2)
                        dve.wait_ge(wprod_hi, L * 8 + (4 * n + 2 * r + odd + 1))
                        nc.vector.scalar_tensor_tensor(out=a_lo[0:E, heads, :], in0=src, scalar=DH ** -0.5,
                                                       in1=a_hi[0:E, heads, :].bitcast(F32), op0=ALU.mult,
                                                       op1=ALU.subtract).then_inc(wprod_lo, 1)
                dve.wait_ge(wv_hi_s, L * 2 + (n + 1))
                nc.vector.tensor_tensor(wv_lo[0:E, :], raw_v[0:E, :], wv_hi[0:E, :].bitcast(F32),
                                        ALU.subtract).then_inc(wv_lo_s, 1)

                def group_in(g, par):
                    rows_lo(c, groups + g, ph.G, par)
                    if n == 1:
                        dve.wait_ge(c["chi"], groups + g)
                        nc.vector.tensor_tensor(c_lo[:, par, :], craw[:].rearrange("p b j -> p (b j)"),
                                                c_hi[:, par, :].bitcast(F32), ALU.subtract).then_inc(c["clo"], 1)

                def item_lo(it, base, wbase, vbase, v_free):
                    kind, a, z, m, q = it
                    if kind == "w":
                        cols = slice(a * ph.HI * ph.GJ, (a + 1) * ph.HI * ph.GJ)
                        dve.wait_ge(c["whi"], wbase + (q + 1))
                        nc.vector.tensor_tensor(w_lo[:, z, cols], it_ps[m % 2][:, 0:ph.HI * ph.GJ],
                                                w_hi[:, z, cols].bitcast(F32), ALU.subtract).then_inc(c["evac"], 1)
                    else:
                        dve.wait_ge(c["item"], base + (m + 1))
                        if v_free is not None:
                            dve.wait_ge(c["pv"], v_free)
                        nc.vector.tensor_copy(v_sb[0:J, a % VRING, z * PS_BANK:(z + 1) * PS_BANK],
                                              it_ps[m % 2][0:J, :]).then_inc(c["evac"], 1)

                group_in(1, 0)
                dve.wait_ge(wv_lo_s, L * 2 + (n + 1))
                for it in ph.prologue():
                    item_lo(it, items, L * (ph.w_per_group * ph.groups), 0, None)
                plans = {False: ph.body(False), True: ph.body(True)}

                def step(i, s, first, last_body):
                    k = units + (i * ph.UB + s)
                    its = []
                    if exists(ph.UB, s, first, last_body, 0):
                        g, gs = s // ph.U, s % ph.U
                        ib = items + (i * ph.items_per_body + ph.items_prologue)
                        wb = L * (ph.w_per_group * ph.groups) + (i * (2 * ph.w_per_group) + ph.w_per_group)
                        its = plans[last_body][s]

                        def v_free(it):
                            b = it[1]
                            if first and b < VRING:
                                return None
                            return units + (i * ph.UB + (b - VRING + 1) * UPB)
                        dve.wait_ge(c["scores"], k + 1)
                        nc.vector.tensor_reduce(nmax[:, s % PRING, :],
                                                sc_ps[s % 2][:, 0:HG * JP].rearrange("p (h j) -> p h j", h=HG)[:, :, 0:J],
                                                AX.X, ALU.max, negate=True).then_inc(c["nmax"], 1)
                        if gs == 0 and not (last_body and g == 1):
                            rows_norm(c, groups + (i * 2 + g + 1), ph.G, i * (2 * ph.G) + (g + 1) * ph.G)
                        if gs == 1 and not (last_body and g == 1):
                            group_in(i * 2 + g + 2, 1 - g)
                        for it in its[:1]:
                            item_lo(it, ib, wb, 0, v_free(it))
                        dve.wait_ge(c["exps"], k + 1)
                        nc.vector.reciprocal(rrec[:, s % PRING, :], rsum[:, s % PRING, :]).then_inc(c["recips"], 1)
                        for it in its[1:]:
                            item_lo(it, ib, wb, 0, v_free(it))
                    if exists(ph.UB, s, first, last_body, PV_LAG):
                        u = s - PV_LAG
                        b = u // UPB
                        dve.wait_ge(c["pv"], k - PV_LAG + 1)
                        if u % UPB == 0 and not (first and b < 2):
                            dve.wait_ge(c["y"], batches + (i * (2 * ph.G) + b - 1))
                        h2 = (HG // 2) * (u % UPB)
                        nc.vector.tensor_copy(ot[:, b % 2, h2:h2 + HG // 2, :],
                                              ot_ps[:, 0:HG // 2 * P].rearrange("p (c n) -> p c n", n=P)).then_inc(c["ot"], 1)
                    if exists(ph.UB, s, first, last_body, Y_LAG) and (s - Y_LAG) % UPB == UPB - 1:
                        b = (s - Y_LAG) // UPB
                        bl = i * (2 * ph.G) + b
                        residual(c, y_ps[:, 0:P], batches + bl, bl)

                bodies(dve, ph.NI, ph.UB, Y_LAG, step)
                dve.wait_ge(c["xstat"], batches + ph.B)

            def feed_forward(L):
                c = FS
                groups, batches = L * (B // FG), L * B
                statistics(L, 2, None)
                raw_ready(dve, L, 2)
                rows_norm(c, None, FG, 0)
                dve.wait_ge(f1_hi_s, L + 1)
                nc.vector.tensor_tensor(f1_lo, raw_f, f1_hi.bitcast(F32), ALU.subtract).then_inc(f1_lo_s, 1)
                rows_lo(c, groups + 1, FG, 0)

                def step(i, s, first, last_body):
                    g = i * 2 + s
                    u = groups * FC + (i * (2 * FC) + s * FC)
                    if exists(2, s, first, last_body, 0):
                        if not (last_body and s == 1):
                            rows_norm(c, groups + (g + 1), FG, i * (2 * FG) + (s + 1) * FG)
                        for ch in range(FC):
                            dve.wait_ge(c["a"], u + (ch + 1))
                            dve.wait_ge(c["gelu"], u + (ch + 1))
                            if ch == 0 and not (first and s < 2):
                                dve.wait_ge(c["y"], batches + (g - 1) * FG)
                            nc.vector.scalar_tensor_tensor(out=hid[:, s % 2, ch, :], in0=tr_ps[ch % 2][:],
                                                           scalar=fb[:, ch:ch + 1], in1=gel[:, ch, :],
                                                           op0=ALU.add, op1=ALU.mult).then_inc(c["hid"], 1)
                        if not (last_body and s == 1):
                            rows_lo(c, groups + (g + 2), FG, 1 - s)
                    if exists(2, s, first, last_body, 1):
                        for b in range(FG):
                            bl = i * (2 * FG) + (s - 1) * FG + b
                            residual(c, it_ps[b % 2][:, 0:P], batches + bl, bl)

                bodies(dve, FNI, 2, 1, step)
                dve.wait_ge(c["xstat"], batches + B)

            for ph in (*PHASES,):
                S[ph.name]["xstat"] = sem(f"{ph.name}_xstat")
            FS["xstat"] = sem("ff_xstat")
            for L in range(LAYERS):
                for n, ph in enumerate(PHASES):
                    attention(n, ph, L)
                feed_forward(L)


def kernel(**inputs):
    import numpy as np
    import concourse.bacc as bacc
    from concourse.bass_utils import run_bass_kernel_spmd as run

    def a(name):
        return np.asarray(inputs[name])

    L0, L1 = "L0_xattn_", "L1_xattn_"

    def both(f0, f1=None):
        return np.ascontiguousarray(np.stack([f0(L0), (f1 or f0)(L1)]))

    lay = {
        "x": np.ascontiguousarray(a("x")),
        "ctx_t": np.ascontiguousarray(a("ctx_768").transpose(2, 0, 1)),
        "wq_t": both(lambda p: np.stack([a(p + "Wq1").T, a(p + "Wq2").T])),
        "wk_t": both(lambda p: a(p + "Wk1").T),
        "wv": both(lambda p: a(p + "Wv1")),
        "wo": both(lambda p: np.stack([a(p + "Wo1"), a(p + "Wo2")])),
        "bo": both(lambda p: np.stack([a(p + "bo1"), a(p + "bo2"), a(p + "bff2")]),
                   lambda p: np.stack([a(p + "bo1"), a(p + "bo2"), a(p + "bf")])),
        "wk2_t": both(lambda p: a(p + "Wk2").T),
        "wv2": both(lambda p: a(p + "Wv2")),
        "ln_g": both(lambda p: np.stack([np.stack([a(f"{p}ln{n}_g"), a(f"{p}ln{n}_b")], -1) for n in (1, 2, 3)]),
                     lambda p: np.stack([np.stack([a(f"{p}g{n}"), a(f"{p}b{n}")], -1) for n in (1, 2, 3)])),
        "ln_b": np.zeros((1, 2), np.float32),
        "w1": both(lambda p: a(p + "Wff1"), lambda p: a(p + "Wp")),
        "b1": both(lambda p: a(p + "bff1").reshape(-1, P).T, lambda p: a(p + "bp").reshape(-1, P).T),
        "w2": both(lambda p: a(p + "Wff2"), lambda p: a(p + "Wf")),
    }
    del lay["ln_b"]
    nc = bacc.Bacc("TRN2", target_bir_lowering=False, num_devices=1)
    aps = {k: nc.dram_tensor("in_" + k, v.shape, mybir.dt.from_np(v.dtype), kind="ExternalInput").ap() for k, v in lay.items()}
    y = nc.dram_tensor("out_y", lay["x"].shape, F32, kind="ExternalOutput").ap()
    block_kernel(nc, aps["x"], aps["ctx_t"], aps["wq_t"], aps["wk_t"], aps["wv"], aps["wo"], aps["bo"],
                 aps["wk2_t"], aps["wv2"], aps["ln_g"], None, aps["w1"], aps["b1"], aps["w2"], y)
    r = run(nc, [{"in_" + k: v for k, v in lay.items()}], core_ids=[0])
    return r.results[0]["out_y"]
```

```python
from contextlib import ExitStack

import concourse.bass as bass
from concourse import mybir

F32 = mybir.dt.float32
F32R = mybir.dt.float32r
ALU = mybir.AluOpType
ACT = mybir.ActivationFunctionType
AX = mybir.AxisListType

P = 128
HEADS, DH = 16, 64
INNER = HEADS * DH
CHUNKS = INNER // P
HG = 4
UPB = HEADS // HG
LAYERS = 2
EPS = 1e-5
PS_BANK = 512
VRING = 4
PRING = 4
EXP_LAG, T_LAG, PV_LAG, Y_LAG = 1, 3, 4, 5
IBANKS = 3


class Attention:

    def __init__(self, name, batches, group, keys, kv_dim, heads_per_item, w_steps):
        self.name, self.B, self.G, self.J, self.E = name, batches, group, keys, kv_dim
        self.JP = keys + keys % 2
        self.GJ = group * self.JP
        self.HI = heads_per_item
        self.U = UPB * group
        self.UB = 2 * self.U
        self.NI = batches // (2 * group)
        self.groups = batches // group
        self.units = UPB * batches
        self.w_per_group = HEADS // heads_per_item
        self.plan = []
        rest = list(range(self.w_per_group))
        for s in range(self.U):
            here = [("v", s // UPB, s % UPB)] if s % UPB < 2 else []
            here += [("w", rest.pop(0)) for _ in range(w_steps[s])]
            self.plan.append(here)
        assert not rest
        self.v_ahead = 1
        self.items_per_body = 2 * (self.w_per_group + 2 * group)
        self.items_prologue = self.w_per_group + 2 * self.v_ahead
        self.items = self.w_per_group * self.groups + 2 * batches

    def body(self, last):
        out, n, w, v = [[] for _ in range(self.UB)], 0, 0, 0
        for s in range(self.UB):
            for it in self.plan[s % self.U]:
                if it[0] == "w":
                    if last and s >= self.U:
                        continue
                    out[s].append(("w", it[1], 1 - s // self.U, n, w))
                    w += 1
                else:
                    b = s // UPB + self.v_ahead
                    if last and b >= 2 * self.G:
                        continue
                    out[s].append(("v", b, it[2], n, v))
                    v += 1
                n += 1
        return out

    def v_count(self, i, b, first, last):
        if b < self.v_ahead:
            if first:
                return self.w_per_group + 2 * b + 2
            plan, off = self.body(False), b + 2 * self.G
            n = next(it[3] for s in plan for it in s if it[:3] == ("v", off, 1)) - self.items_per_body
        else:
            n = next(it[3] for s in self.body(last) for it in s if it[:3] == ("v", b, 1))
        return i * self.items_per_body + (self.items_prologue + n + 1)

    def w_count(self, i, s, first, last):
        g, item = s // self.U, (HG * (s % self.U) + HG - 1) // self.HI
        if g == 0:
            if first:
                return item + 1
            n = next(it[3] for st in self.body(False)[self.U:] for it in st if it[:2] == ("w", item)) - self.items_per_body
        else:
            n = next(it[3] for st in self.body(last)[:self.U] for it in st if it[:2] == ("w", item))
        return i * self.items_per_body + (self.items_prologue + n + 1)

    def prologue(self):
        out = [("w", j, 0, j, j) for j in range(self.w_per_group)]
        for b in range(self.v_ahead):
            for half in range(2):
                v = 2 * b + half
                out.append(("v", b, half, self.w_per_group + v, v))
        return out


def block_kernel(nc, x_in, ctx_t, wq_t, wk_t, wv, wo, bo, wk2_t, wv2, ln_g, ln_b, w1, b1, w2, out):
    B = x_in.shape[0]
    J2 = ctx_t.shape[2]
    E2 = ctx_t.shape[0]
    FF = w1.shape[2] // 2
    FC = FF // P
    FG = 4
    FN = FG * P
    FNI = B // (2 * FG)
    SELF = Attention("self", B, 2, P, P, 2, [0, 0, 1, 2, 1, 1, 1, 2])
    CROSS = Attention("ctx", B, 4, J2, E2, 1, [0, 0, 1, 2, 1, 1, 1, 2] + 2 * [0, 1, 1, 2])
    PHASES = (SELF, CROSS)
    GMAX = 4

    ctx = ExitStack()
    with ctx:
        def sb(name, shape, dt=F32):
            return ctx.enter_context(nc.sbuf_tensor(name, shape, dt))

        def sem(name):
            return ctx.enter_context(nc.semaphore(name))

        x = sb("x", [P, B, P])
        stats = sb("stats", [P, B, 6])
        rstd = sb("rstd", [P, B])
        nmr = sb("nmr", [P, B])
        ident = sb("ident", [P, P])
        xn = sb("xn", [P, GMAX, P])
        xfull = sb("xfull", [P, GMAX * P])
        xt_hi = sb("xt_hi", [P, 2, GMAX * P], F32R)
        xt_lo = sb("xt_lo", [P, 2, GMAX * P], F32R)
        c_hi = sb("c_hi", [E2, 2, CROSS.GJ], F32R)
        c_lo = sb("c_lo", [E2, 2, CROSS.GJ], F32R)
        a_hi = sb("a_hi", [P, HEADS, P], F32R)
        a_lo = sb("a_lo", [P, HEADS, P], F32R)
        wv_hi = sb("wv_hi", [P, INNER], F32R)
        wv_lo = sb("wv_lo", [P, INNER], F32R)
        wo_sb = sb("wo_sb", [P, CHUNKS, P])
        bo_bc = sb("bo_bc", [P, P])
        gb = sb("gb", [P, 3, 2])
        raw = sb("raw", [P, 2, INNER])
        w_hi = sb("w_hi", [P, 2, HEADS * CROSS.GJ], F32R)
        w_lo = sb("w_lo", [P, 2, HEADS * CROSS.GJ], F32R)
        v_sb = sb("v_sb", [P, VRING, INNER])
        probs = sb("probs", [P, PRING, HG, P])
        nmax = sb("nmax", [P, PRING, HG])
        rsum = sb("rsum", [P, PRING, HG])
        rrec = sb("rrec", [P, PRING, HG])
        pt = sb("pt", [P, 2, HG * P])
        ot = sb("ot", [P, 2, CHUNKS, P])
        ytmp = sb("ytmp", [P, P])
        fb = sb("fb", [P, 2 * FC])
        raw_q, raw_k = raw[:, 0, :], raw[:, 1, :]
        raw_v = v_sb[:, VRING - 1, :]
        f2_sb = wo_sb[:, 0:FC, :]
        craw = raw[0:E2, 1, 0:CROSS.GJ].rearrange("p (b j) -> p b j", b=GMAX)
        lnst = xfull[:, 0:6 * B].rearrange("p (s b) -> p s b", s=6)
        f1_hi = a_hi[:, 0:2 * FC, :].rearrange("p c n -> p (c n)")
        f1_lo = a_lo[:, 0:2 * FC, :].rearrange("p c n -> p (c n)")
        gel = probs[:].rearrange("p a b c -> p a (b c)")
        raw_f = raw[:, 0, :]
        hid = v_sb[:].rearrange("p (a b) (c n) -> p a (b c) n", a=2, n=FN)

        def bank(name):
            return ctx.enter_context(nc.psum_tensor(name, [P, PS_BANK], F32))
        sc_ps = [bank(f"sc_ps{i}") for i in range(2)]
        tr_ps = bank("tr_ps")
        it_ps = [bank(f"it_ps{i}") for i in range(IBANKS)]
        ot_ps = bank("ot_ps")
        y_ps = bank("y_ps")

        x_loaded = [sem(f"x_loaded{i}") for i in range(4)]
        x_stats0 = sem("x_stats0")
        ident_zero, ident_ready = sem("ident_zero"), sem("ident_ready")
        chain = sem("chain")
        var_ready, std_ready = sem("var_ready"), sem("std_ready")
        phase_open = sem("phase_open")
        raw_in = sem("raw_in")
        raw_v_in = sem("raw_v_in")
        ln_in = [sem(f"ln_in{n}") for n in range(3)]
        par_in = sem("par_in")
        wprod_ps, wprod_hi, wprod_lo = sem("wprod_ps"), sem("wprod_hi"), sem("wprod_lo")
        wv_hi_s, wv_lo_s = sem("wv_hi_s"), sem("wv_lo_s")
        f1_hi_s, f1_lo_s = sem("f1_hi_s"), sem("f1_lo_s")
        out_done = sem("out_done")
        S = {}
        for ph in PHASES:
            S[ph.name] = {k: sem(f"{ph.name}_{k}") for k in (
                "scores", "nmax", "exps", "recips", "normed", "turned", "pt", "pv", "ot", "y", "ysum",
                "resid", "item", "whi", "evac", "xn", "xnT", "xhi", "xfull", "xlo", "craw", "chi", "clo")}
        FS = {k: sem(f"ff_{k}") for k in ("xn", "xnT", "xhi", "xfull", "xlo", "gate", "a", "gelu", "hid",
                                          "y", "ysum", "resid")}

        CHAIN = 10
        CHAIN_LAYER = 3 * CHAIN
        RAW_DMAS = (2, 2, 1)
        LN_DMAS = (1, 1, 2)

        def open_phase(eng, L, n):
            eng.wait_ge(phase_open, L * 3 + (n + 1))

        def batch_of(i, ph_or_g, b):
            return i * (2 * ph_or_g) + b

        block = ctx.enter_context(nc.Block())

        def bodies(eng, NI, steps, lag, step):
            for s in range(steps):
                step(0, s, True, False)
            with eng.Fori(1, NI - 1) as i:
                for s in range(steps):
                    step(i, s, False, False)
            for s in range(steps + lag):
                step(NI - 1, s, False, True)

        def exists(ph_steps, s, first, last, lag):
            return not (first and s < lag) and not (last and s - lag >= ph_steps)

        @block.sync
        def _(sp):
            q = B // 4
            for c in range(4):
                sp.dma_start(x[:, c * q:(c + 1) * q, :],
                             x_in[c * q:(c + 1) * q].rearrange("b t d -> t b d")).then_inc(x_loaded[c], 16)
            for L in range(LAYERS):
                for n in range(3):
                    prev = L * 3 + n
                    if prev and n != 0:
                        sp.wait_ge(wprod_ps, L * 4 + 2 * n)
                    elif prev:
                        sp.wait_ge(f1_lo_s, L)
                    if n < 2:
                        ph, kt, vv = (SELF, wk_t, wv) if n == 0 else (CROSS, wk2_t, wv2)
                        E = ph.E
                        sp.dma_start(raw_q.rearrange("p (c n) -> p c n", c=CHUNKS),
                                     wq_t[L, n].rearrange("(c p) n -> p c n", p=P)).then_inc(raw_in, 16)
                        sp.dma_start(raw_k[:, 0:CHUNKS * E].rearrange("p (c n) -> p c n", c=CHUNKS),
                                     kt[L].rearrange("(c p) n -> p c n", p=P)).then_inc(raw_in, 16)
                    else:
                        sp.dma_start(raw_f, w1[L]).then_inc(raw_in, 16)
                        sp.dma_start(fb[:], b1[L]).then_inc(ln_in[n], 16)
                    sp.dma_start(gb[:, n, :], ln_g[L, n]).then_inc(ln_in[n], 16)
                    if n < 2:
                        if n == 1:
                            sp.wait_ge(S["self"]["pv"], (L + 1) * SELF.units)
                        elif prev:
                            sp.wait_ge(FS["y"], L * B)
                        sp.dma_start(raw_v[0:E, :], vv[L]).then_inc(raw_v_in, 16)
                    sp.wait_ge(phase_open, L * 3 + n + 1)
                    if n < 2:
                        sp.dma_start(wo_sb[:], wo[L, n].rearrange("(c p) n -> p c n", p=P)).then_inc(par_in, 16)
                    else:
                        sp.dma_start(f2_sb, w2[L].rearrange("(c p) n -> p c n", p=P)).then_inc(par_in, 16)
                    sp.dma_start(bo_bc[:], bo[L, n:n + 1, :].to_broadcast([P, P])).then_inc(par_in, 16)
                    if n == 1:
                        c = S[ph.name]
                        sp.wait_ge(wprod_ps, L * 4 + 4)
                        sp.dma_start(craw[:, :, 0:J2], ctx_t[:, 0:ph.G, :]).then_inc(c["craw"], 16)
                        with sp.Fori(1, ph.groups) as g:
                            sp.wait_ge(c["clo"], L * ph.groups + g)
                            sp.dma_start(craw[:, :, 0:J2], ctx_t[:, bass.ts(g, ph.G), :]).then_inc(c["craw"], 16)
            sp.wait_ge(FS["resid"], LAYERS * B)
            for c in range(4):
                sp.dma_start(out[c * q:(c + 1) * q].rearrange("b t d -> t b d"),
                             x[:, c * q:(c + 1) * q, :]).then_inc(out_done, 16)
            sp.wait_ge(out_done, 64)

        def raw_ready(eng, L, n):
            eng.wait_ge(raw_in, 16 * (L * sum(RAW_DMAS) + sum(RAW_DMAS[:n + 1])))

        def ln_ready(eng, L, n):
            eng.wait_ge(ln_in[n], 16 * (L + 1) * LN_DMAS[n])

        def par_ready(eng, L, n):
            eng.wait_ge(par_in, 16 * 2 * (L * 3 + n + 1))

        @block.gpsimd
        def _(pool):
            nc.gpsimd.memset(ident[:], 0.0).then_inc(ident_zero, 1)
            pool.wait_ge(ident_zero, 1)
            nc.gpsimd.affine_select(out=ident[:], in_=ident[:], compare_op=ALU.not_equal, fill=1.0,
                                    base=0, pattern=[[-1, P]], channel_multiplier=1).then_inc(ident_ready, 1)

            def phase(ph, L):
                c = S[ph.name]
                base = L * ph.units

                def step(i, s, first, last):
                    if not exists(ph.UB, s, first, last, 0):
                        return
                    k = base + (i * ph.UB + s)
                    pr = probs[:, s % PRING, :, 0:ph.J]
                    pool.wait_ge(c["recips"], k + 1)
                    nc.gpsimd.tensor_tensor(pr, pr, rrec[:, s % PRING, :].unsqueeze(2).to_broadcast([P, HG, ph.J]),
                                            ALU.mult).then_inc(c["normed"], 1)

                bodies(pool, ph.NI, ph.UB, 0, step)

            for L in range(LAYERS):
                for ph in PHASES:
                    phase(ph, L)

        @block.tensor
        def _(pe):
            def three(out_, l_hi, l_lo, r_hi, r_lo):
                nc.tensor.matmul(out_, l_hi, r_hi, start=True, stop=False)
                nc.tensor.matmul(out_, l_hi, r_lo, start=False, stop=False)
                return nc.tensor.matmul(out_, l_lo, r_hi, start=False, stop=True)

            def turn_rows(c, g_count, G, free_wait):
                pe.wait_ge(c["xn"], g_count)
                for wsem, val in free_wait:
                    pe.wait_ge(wsem, val)
                for b in range(G):
                    last = nc.tensor.transpose(y_ps[:, b * P:(b + 1) * P], xn[:, b, :], ident[:])
                last.then_inc(c["xnT"], 1)

            def attention(n, ph, L):
                c = S[ph.name]
                E, J, JP = ph.E, ph.J, ph.JP
                units, items, groups, batches = L * ph.units, L * ph.items, L * ph.groups, L * ph.B
                raw_ready(pe, L, n)
                if n == 0 and L:
                    pe.wait_ge(FS["hid"], L * (B // FG) * FC)
                if n == 1:
                    pe.wait_ge(S["self"]["evac"], (L + 1) * SELF.items)
                for r in range(2):
                    for j in range(4):
                        for odd in range(2):
                            h = 8 * r + 2 * j + odd
                            rows = slice(DH * odd, DH * odd + DH)
                            last = nc.tensor.matmul(
                                (sc_ps if r == 0 else it_ps)[odd][0:E, j * P:(j + 1) * P],
                                raw_k[rows, (h // 2) * E:(h // 2 + 1) * E],
                                raw_q[rows, (h // 2) * P:(h // 2 + 1) * P], start=True, stop=True)
                    last.then_inc(wprod_ps, 1)
                open_phase(pe, L, n)

                def kv(par, b=None):
                    hi, lo = (xt_hi, xt_lo) if n == 0 else (c_hi, c_lo)
                    if b is None:
                        return hi[0:E, par, 0:ph.GJ], lo[0:E, par, 0:ph.GJ]
                    return hi[0:E, par, b * JP:b * JP + J], lo[0:E, par, b * JP:b * JP + J]

                def item(it, base, off):
                    kind, a, z, m, q = it
                    dst = it_ps[(m + off) % IBANKS]
                    if m + off >= IBANKS:
                        pe.wait_ge(c["evac"], base + (m + 1 - IBANKS))
                    if kind == "w":
                        hi, lo = kv(z)
                        for t in range(ph.HI):
                            h = a * ph.HI + t
                            last = three(dst[:, t * ph.GJ:(t + 1) * ph.GJ], a_hi[0:E, h, :], a_lo[0:E, h, :], hi, lo)
                    else:
                        hi, lo = kv((a // ph.G) % 2, a % ph.G)
                        cols = slice(z * PS_BANK, (z + 1) * PS_BANK)
                        last = three(dst[0:J, :], hi, lo, wv_hi[0:E, cols], wv_lo[0:E, cols])
                    last.then_inc(c["item"], 1)

                def kv_ready(g):
                    pe.wait_ge(c["xlo"], groups + g)
                    if n == 1:
                        pe.wait_ge(c["clo"], groups + g)

                turn_rows(c, groups + 1, ph.G, ())
                pe.wait_ge(wprod_lo, L * 8 + (4 * n + 4))
                pe.wait_ge(wv_lo_s, L * 2 + (n + 1))
                kv_ready(1)
                for it in ph.prologue():
                    item(it, items, 0)
                par_ready(pe, L, n)
                plans = {False: ph.body(False), True: ph.body(True)}

                def step(i, s, first, last_body):
                    k = units + (i * ph.UB + s)
                    if exists(ph.UB, s, first, last_body, 0):
                        g, gs, b = s // ph.U, s % ph.U, s // UPB
                        if gs < UPB:
                            pe.wait_ge(c["evac"], items + ph.w_count(i, s, first, last_body))
                        if not (first and s < 2):
                            pe.wait_ge(c["exps"], k - 1)
                        bank_ = sc_ps[s % 2][:, 0:HG * JP]
                        h0 = HG * (s % UPB)
                        bg = b % ph.G
                        rows = slice(bg * P, (bg + 1) * P)

                        def w(t):
                            return t[:, g % 2, 0:HEADS * ph.GJ].rearrange("p (h j) -> p h j", h=HEADS)[
                                :, h0:h0 + HG, bg * JP:(bg + 1) * JP]
                        three(bank_, xt_hi[:, g % 2, rows], xt_lo[:, g % 2, rows], w(w_hi), w(w_lo)).then_inc(c["scores"], 1)
                        its = plans[last_body][s]
                        ib = items + (i * ph.items_per_body + ph.items_prologue)
                        early = 0 if gs == 2 else 1
                        for it in its[:early]:
                            item(it, ib, ph.items_prologue)
                    else:
                        its = []
                    if exists(ph.UB, s, first, last_body, T_LAG):
                        u = s - T_LAG
                        pe.wait_ge(c["normed"], k - T_LAG + 1)
                        if not (first and u < 1):
                            pe.wait_ge(c["pt"], k - T_LAG)
                        for t in range(HG):
                            last = nc.tensor.transpose(tr_ps[0:J, t * P:(t + 1) * P],
                                                       probs[:, u % PRING, t, 0:J], ident[:])
                        last.then_inc(c["turned"], 1)
                    if its or s < ph.UB and s % ph.U == 1:
                        more = not (last_body and g == 1)
                        if gs == 1 and more:
                            bd = i * (2 * ph.G) + g * ph.G
                            fw = () if first and g == 0 else ((c["ysum"], batches + (bd - 1)),)
                            turn_rows(c, groups + (i * 2 + g + 2), ph.G, fw)
                        if gs == 2 and more:
                            kv_ready(i * 2 + g + 2)
                    for it in its[early if its else 0:]:
                        item(it, ib, ph.items_prologue)
                    if exists(ph.UB, s, first, last_body, PV_LAG):
                        u = s - PV_LAG
                        b = u // UPB
                        pe.wait_ge(c["pt"], k - PV_LAG + 1)
                        if not (first and u < 1):
                            pe.wait_ge(c["ot"], k - PV_LAG)
                        if u % UPB == 0:
                            pe.wait_ge(c["evac"], items + ph.v_count(i, b, first, last_body))
                        h0 = HG * (u % UPB)
                        for t in range(HG):
                            o = ot_ps[DH * (t % 2):DH * (t % 2) + DH, (t // 2) * P:(t // 2 + 1) * P]
                            last = nc.tensor.matmul(o, v_sb[0:J, b % VRING, (h0 + t) * DH:(h0 + t + 1) * DH],
                                                    pt[0:J, u % 2, t * P:(t + 1) * P], start=True, stop=True)
                        last.then_inc(c["pv"], 1)
                    if exists(ph.UB, s, first, last_body, Y_LAG) and (s - Y_LAG) % UPB:
                        b, hg = (s - Y_LAG) // UPB, (s - Y_LAG) % UPB
                        bb = batches + (i * (2 * ph.G) + b)
                        pe.wait_ge(c["ot"], k - Y_LAG + 1)
                        if hg == 1:
                            if not (first and b < 1):
                                pe.wait_ge(c["ysum"], bb)
                            turned = 1 + (s + ph.U - 2) // ph.U
                            pe.wait_ge(c["xlo"], groups + (i * 2 + (min(turned, 2) if last_body else turned)))
                        for ch in range(0 if hg == 1 else 2 * hg, 2 * hg + 2):
                            last = nc.tensor.matmul(y_ps[:, 0:P], ot[:, b % 2, ch, :], wo_sb[:, ch, :],
                                                    start=(ch == 0), stop=(ch == CHUNKS - 1))
                        if hg == UPB - 1:
                            last.then_inc(c["y"], 1)

                bodies(pe, ph.NI, ph.UB, Y_LAG, step)

            def feed_forward(L):
                c = FS
                groups, batches = L * (B // FG), L * B
                open_phase(pe, L, 2)
                turn_rows(c, groups + 1, FG, ())
                pe.wait_ge(f1_lo_s, L + 1)
                par_ready(pe, L, 2)

                def step(i, s, first, last_body):
                    g = i * 2 + s
                    u = groups * FC + (i * (2 * FC) + s * FC)
                    if exists(2, s, first, last_body, 0):
                        pe.wait_ge(c["xlo"], groups + (g + 1))
                        hi, lo = xt_hi[:, s % 2, :], xt_lo[:, s % 2, :]
                        for ch in range(FC):
                            ga, aa = sc_ps[ch % 2], it_ps[ch % 2]
                            if not (first and s == 0 and ch < 2):
                                pe.wait_ge(c["gelu"], u + (ch - 1))
                            cols = slice(FF + ch * P, FF + (ch + 1) * P)
                            three(ga[:], f1_hi[:, cols], f1_lo[:, cols], hi, lo).then_inc(c["gate"], 1)
                            if not (first and s == 0 and ch < 2):
                                pe.wait_ge(c["hid"], u + (ch - 1))
                            cols = slice(ch * P, (ch + 1) * P)
                            three(aa[:], f1_hi[:, cols], f1_lo[:, cols], hi, lo).then_inc(c["a"], 1)
                        if not (last_body and s == 1):
                            turn_rows(c, groups + (g + 2), FG, ())
                    if exists(2, s, first, last_body, 1):
                        for b in range(FG):
                            bb = batches + ((g - 1) * FG + b)
                            if b == 0:
                                pe.wait_ge(c["hid"], u)
                            if not (first and s == 1 and b < 2):
                                pe.wait_ge(c["ysum"], bb - 1)
                            for ch in range(FC):
                                last = nc.tensor.matmul((ot_ps, tr_ps)[b % 2][:, 0:P],
                                                        hid[:, (s - 1) % 2, ch, b * P:(b + 1) * P],
                                                        f2_sb[:, ch, :], start=(ch == 0), stop=(ch == FC - 1))
                            last.then_inc(c["y"], 1)

                bodies(pe, FNI, 2, 1, step)

            pe.wait_ge(ident_ready, 1)
            for L in range(LAYERS):
                for n, ph in enumerate(PHASES):
                    attention(n, ph, L)
                feed_forward(L)

        @block.scalar
        def _(act):
            def std(L, n):
                act.wait_ge(var_ready, L * 3 + (n + 1))
                nc.scalar.activation(lnst[:, 4, :], lnst[:, 3, :], ACT.Sqrt).then_inc(std_ready, 1)

            def rows_hi(c, n, count, G, par):
                act.wait_ge(c["xnT"], count)
                nc.scalar.activation(xt_hi[:, par, 0:G * P], y_ps[:, 0:G * P], ACT.Identity,
                                     scale=gb[:, n, 0:1], bias=gb[:, n, 1:2]).then_inc(c["xhi"], 1)

            def attention(n, ph, L):
                c = S[ph.name]
                E, J, JP = ph.E, ph.J, ph.JP
                units, items, groups = L * ph.units, L * ph.items, L * ph.groups
                raw_ready(act, L, n)
                if L or n:
                    pw, pv_ = (FS["a"], L * (B // FG) * FC) if n == 0 else (S["self"]["item"], (L + 1) * SELF.items)
                    act.wait_ge(pw, pv_)
                for r in range(2):
                    act.wait_ge(wprod_ps, L * 4 + (2 * n + r + 1))
                    for odd in range(2):
                        src = (sc_ps if r == 0 else it_ps)[odd][0:E, :].rearrange("p (h n) -> p h n", h=4)
                        nc.scalar.activation(a_hi[0:E, 8 * r + odd:8 * r + 8:2, :], src, ACT.Copy,
                                             scale=DH ** -0.5).then_inc(wprod_hi, 1)
                std(L, n)
                act.wait_ge(raw_v_in, 16 * (2 * L + n + 1))
                nc.scalar.copy(wv_hi[0:E, :], raw_v[0:E, :]).then_inc(wv_hi_s, 1)
                open_phase(act, L, n)
                ln_ready(act, L, n)

                def group_in(g, par):
                    rows_hi(c, n, groups + g, ph.G, par)
                    if n == 1:
                        act.wait_ge(c["craw"], groups * 16 + g * 16)
                        nc.scalar.copy(c_hi[:, par, :], craw[:].rearrange("p b j -> p (b j)")).then_inc(c["chi"], 1)

                def item_hi(it, base, off):
                    kind, a, z, m, q = it
                    if kind == "w":
                        act.wait_ge(c["item"], base + (m + 1))
                        nc.scalar.copy(w_hi[:, z, a * ph.HI * ph.GJ:(a + 1) * ph.HI * ph.GJ],
                                       it_ps[(m + off) % IBANKS][:, 0:ph.HI * ph.GJ]).then_inc(c["whi"], 1)

                group_in(1, 0)
                for it in ph.prologue():
                    item_hi(it, items, 0)
                plans = {False: ph.body(False), True: ph.body(True)}

                def step(i, s, first, last_body):
                    k = units + (i * ph.UB + s)
                    its = []
                    if exists(ph.UB, s, first, last_body, 0):
                        g, gs = s // ph.U, s % ph.U
                        ib = items + (i * ph.items_per_body + ph.items_prologue)
                        its = plans[last_body][s]
                    if exists(ph.UB, s, first, last_body, EXP_LAG):
                        u = s - EXP_LAG
                        act.wait_ge(c["nmax"], k - EXP_LAG + 1)
                        if not (first and u < PRING):
                            act.wait_ge(c["turned"], k - EXP_LAG - PRING + 1)
                        for t in range(HG):
                            last = nc.scalar.activation(
                                probs[:, u % PRING, t, 0:J], sc_ps[u % 2][:, t * JP:t * JP + J], ACT.Exp,
                                bias=nmax[:, u % PRING, t:t + 1], scale=1.0,
                                accum_out=rsum[:, u % PRING, t:t + 1])
                        last.then_inc(c["exps"], 1)
                    for it in its[:1]:
                        item_hi(it, ib, ph.items_prologue)
                    if exists(ph.UB, s, first, last_body, T_LAG):
                        u = s - T_LAG
                        act.wait_ge(c["turned"], k - T_LAG + 1)
                        if not (first and u < 2):
                            act.wait_ge(c["pv"], k - T_LAG - 1)
                        nc.scalar.copy(pt[0:J, u % 2, :], tr_ps[0:J, :]).then_inc(c["pt"], 1)
                    for it in its[1:]:
                        item_hi(it, ib, ph.items_prologue)
                    if s < ph.UB and gs == 1 and not (last_body and g == 1):
                        group_in(i * 2 + g + 2, 1 - g)

                bodies(act, ph.NI, ph.UB, T_LAG, step)

            def feed_forward(L):
                c = FS
                groups = L * (B // FG)
                raw_ready(act, L, 2)
                act.wait_ge(S["ctx"]["item"], (L + 1) * CROSS.items)
                nc.scalar.copy(f1_hi, raw_f).then_inc(f1_hi_s, 1)
                std(L, 2)
                open_phase(act, L, 2)
                ln_ready(act, L, 2)
                rows_hi(c, 2, groups + 1, FG, 0)

                def step(i, s, first, last_body):
                    if not exists(2, s, first, last_body, 0):
                        return
                    u = groups * FC + (i * (2 * FC) + s * FC)
                    for ch in range(FC):
                        act.wait_ge(c["gate"], u + (ch + 1))
                        if not (first and s == 0):
                            act.wait_ge(c["hid"], u + (ch + 1 - FC))
                        nc.scalar.activation(gel[:, ch, :], sc_ps[ch % 2][:], ACT.Gelu,
                                             bias=fb[:, FC + ch:FC + ch + 1], scale=1.0).then_inc(c["gelu"], 1)
                    if not (last_body and s == 1):
                        rows_hi(c, 2, groups + (i * 2 + s + 2), FG, 1 - s)

                bodies(act, FNI, 2, 0, step)

            for L in range(LAYERS):
                for n, ph in enumerate(PHASES):
                    attention(n, ph, L)
                feed_forward(L)

        @block.vector
        def _(dve):
            for b in range(B):
                if b % (B // 4) == 0:
                    dve.wait_ge(x_loaded[b // (B // 4)], 16)
                last = nc.vector.bn_stats(stats[:, b, :], x[:, b, :])
            last.then_inc(x_stats0, 1)
            dve.wait_ge(x_stats0, 1)

            def statistics(L, n, prev):
                base = L * CHAIN_LAYER + n * CHAIN
                done = [0]

                def link(ins):
                    done[0] += 1
                    ins.then_inc(chain, 1)
                    dve.wait_ge(chain, base + done[0])

                me, qe, mo, qo = (stats[:, :, j] for j in (1, 2, 4, 5))
                total, diff, q, var, sd, t = (lnst[:, j, :] for j in range(6))
                link(nc.vector.tensor_tensor(total, me, mo, ALU.add))
                link(nc.vector.tensor_tensor(diff, me, mo, ALU.subtract))
                link(nc.vector.tensor_tensor(q, qe, qo, ALU.add))
                link(nc.vector.tensor_tensor(diff, diff, diff, ALU.mult))
                link(nc.vector.scalar_tensor_tensor(out=q, in0=diff, scalar=P / 4.0, in1=q, op0=ALU.mult, op1=ALU.add))
                nc.vector.tensor_scalar(var, q, 1.0 / P, EPS, ALU.mult, ALU.add).then_inc(var_ready, 1)
                dve.wait_ge(std_ready, L * 3 + (n + 1))
                link(nc.vector.reciprocal(rstd[:], sd))
                link(nc.vector.tensor_tensor(t, rstd[:], rstd[:], ALU.mult))
                link(nc.vector.tensor_tensor(t, t, var, ALU.mult))
                link(nc.vector.tensor_scalar(t, t, -0.5, 1.5, ALU.mult, ALU.add))
                link(nc.vector.tensor_tensor(rstd[:], rstd[:], t, ALU.mult))
                assert done[0] == CHAIN
                nc.vector.scalar_tensor_tensor(out=nmr[:], in0=total, scalar=-0.5, in1=rstd[:],
                                               op0=ALU.mult, op1=ALU.mult).then_inc(phase_open, 1)
                dve.wait_ge(phase_open, L * 3 + (n + 1))

            def rows_norm(c, count, G, b0):
                for b in range(G):
                    bb = b0 + b
                    if b == 0 and count is not None:
                        dve.wait_ge(c["xnT"], count)
                    ins = nc.vector.tensor_scalar(xn[:, b, :], x[:, bb, :], rstd[:, bass.ds(bb, 1)],
                                                  nmr[:, bass.ds(bb, 1)], ALU.mult, ALU.add)
                ins.then_inc(c["xn"], 1)

            def rows_lo(c, n, count, G, par):
                dve.wait_ge(c["xnT"], count)
                dve.wait_ge(c["xhi"], count)
                nc.vector.tensor_scalar(xfull[:, 0:G * P], y_ps[:, 0:G * P], gb[:, n, 0:1], gb[:, n, 1:2],
                                        ALU.mult, ALU.add).then_inc(c["xfull"], 1)
                dve.wait_ge(c["xfull"], count)
                nc.vector.tensor_tensor(xt_lo[:, par, 0:G * P], xfull[:, 0:G * P],
                                        xt_hi[:, par, 0:G * P].bitcast(F32), ALU.subtract).then_inc(c["xlo"], 1)

            def residual(c, n, src, bb, b):
                dve.wait_ge(c["y"], bb + 1)
                nc.vector.tensor_tensor(ytmp[:], src, bo_bc[:], ALU.add).then_inc(c["ysum"], 1)
                dve.wait_ge(c["ysum"], bb + 1)
                nc.vector.tensor_tensor(x[:, b, :], x[:, b, :], ytmp[:], ALU.add).then_inc(c["resid"], 1)
                dve.wait_ge(c["resid"], bb + 1)
                nc.vector.bn_stats(stats[:, b, :], x[:, b, :]).then_inc(c["xstat"], 1)

            def attention(n, ph, L):
                c = S[ph.name]
                E, J, JP = ph.E, ph.J, ph.JP
                units, items, groups, batches = L * ph.units, L * ph.items, L * ph.groups, L * ph.B
                statistics(L, n, None)
                ln_ready(dve, L, n)
                rows_norm(c, None, ph.G, 0)
                for r in range(2):
                    for odd in range(2):
                        src = (sc_ps if r == 0 else it_ps)[odd][0:E, :].rearrange("p (h n) -> p h n", h=4)
                        heads = slice(8 * r + odd, 8 * r + 8, 2)
                        dve.wait_ge(wprod_hi, L * 8 + (4 * n + 2 * r + odd + 1))
                        nc.vector.scalar_tensor_tensor(out=a_lo[0:E, heads, :], in0=src, scalar=DH ** -0.5,
                                                       in1=a_hi[0:E, heads, :].bitcast(F32), op0=ALU.mult,
                                                       op1=ALU.subtract).then_inc(wprod_lo, 1)
                dve.wait_ge(wv_hi_s, L * 2 + (n + 1))
                nc.vector.tensor_tensor(wv_lo[0:E, :], raw_v[0:E, :], wv_hi[0:E, :].bitcast(F32),
                                        ALU.subtract).then_inc(wv_lo_s, 1)

                def group_in(g, par):
                    rows_lo(c, n, groups + g, ph.G, par)
                    if n == 1:
                        dve.wait_ge(c["chi"], groups + g)
                        nc.vector.tensor_tensor(c_lo[:, par, :], craw[:].rearrange("p b j -> p (b j)"),
                                                c_hi[:, par, :].bitcast(F32), ALU.subtract).then_inc(c["clo"], 1)

                def item_lo(it, base, wbase, off, v_free):
                    kind, a, z, m, q = it
                    if kind == "w":
                        cols = slice(a * ph.HI * ph.GJ, (a + 1) * ph.HI * ph.GJ)
                        dve.wait_ge(c["whi"], wbase + (q + 1))
                        nc.vector.tensor_tensor(w_lo[:, z, cols], it_ps[(m + off) % IBANKS][:, 0:ph.HI * ph.GJ],
                                                w_hi[:, z, cols].bitcast(F32), ALU.subtract).then_inc(c["evac"], 1)
                    else:
                        dve.wait_ge(c["item"], base + (m + 1))
                        if v_free is not None:
                            dve.wait_ge(c["pv"], v_free)
                        nc.vector.tensor_copy(v_sb[0:J, a % VRING, z * PS_BANK:(z + 1) * PS_BANK],
                                              it_ps[(m + off) % IBANKS][0:J, :]).then_inc(c["evac"], 1)

                group_in(1, 0)
                par_ready(dve, L, n)
                dve.wait_ge(wv_lo_s, L * 2 + (n + 1))
                for it in ph.prologue():
                    item_lo(it, items, L * (ph.w_per_group * ph.groups), 0, None)
                plans = {False: ph.body(False), True: ph.body(True)}

                def step(i, s, first, last_body):
                    k = units + (i * ph.UB + s)
                    its = []
                    if exists(ph.UB, s, first, last_body, 0):
                        g, gs = s // ph.U, s % ph.U
                        ib = items + (i * ph.items_per_body + ph.items_prologue)
                        wb = L * (ph.w_per_group * ph.groups) + (i * (2 * ph.w_per_group) + ph.w_per_group)
                        its = plans[last_body][s]

                        def v_free(it):
                            b = it[1]
                            if first and b < VRING:
                                return None
                            return units + (i * ph.UB + (b - VRING + 1) * UPB)
                        dve.wait_ge(c["scores"], k + 1)
                        nc.vector.tensor_reduce(nmax[:, s % PRING, :],
                                                sc_ps[s % 2][:, 0:HG * JP].rearrange("p (h j) -> p h j", h=HG)[:, :, 0:J],
                                                AX.X, ALU.max, negate=True).then_inc(c["nmax"], 1)
                        if gs == 0 and not (last_body and g == 1):
                            rows_norm(c, groups + (i * 2 + g + 1), ph.G, i * (2 * ph.G) + (g + 1) * ph.G)
                        for it in its[:1]:
                            item_lo(it, ib, wb, ph.items_prologue, v_free(it))
                    if exists(ph.UB, s, first, last_body, EXP_LAG):
                        u = s - EXP_LAG
                        dve.wait_ge(c["exps"], k - EXP_LAG + 1)
                        nc.vector.reciprocal(rrec[:, u % PRING, :], rsum[:, u % PRING, :]).then_inc(c["recips"], 1)
                    for it in its[1:]:
                        item_lo(it, ib, wb, ph.items_prologue, v_free(it))
                    if exists(ph.UB, s, first, last_body, PV_LAG):
                        u = s - PV_LAG
                        b = u // UPB
                        dve.wait_ge(c["pv"], k - PV_LAG + 1)
                        if u % UPB == 0 and not (first and b < 2):
                            dve.wait_ge(c["y"], batches + (i * (2 * ph.G) + b - 1))
                        h2 = (HG // 2) * (u % UPB)
                        nc.vector.tensor_copy(ot[:, b % 2, h2:h2 + HG // 2, :],
                                              ot_ps[:, 0:HG // 2 * P].rearrange("p (c n) -> p c n", n=P)).then_inc(c["ot"], 1)
                    if exists(ph.UB, s, first, last_body, Y_LAG) and (s - Y_LAG) % UPB == UPB - 1:
                        b = (s - Y_LAG) // UPB
                        bl = i * (2 * ph.G) + b
                        residual(c, n, y_ps[:, 0:P], batches + bl, bl)
                    if s < ph.UB and gs == 1 and not (last_body and g == 1):
                        group_in(i * 2 + g + 2, 1 - g)

                bodies(dve, ph.NI, ph.UB, Y_LAG, step)
                dve.wait_ge(c["xstat"], batches + ph.B)

            def feed_forward(L):
                c = FS
                groups, batches = L * (B // FG), L * B
                statistics(L, 2, None)
                ln_ready(dve, L, 2)
                rows_norm(c, None, FG, 0)
                dve.wait_ge(f1_hi_s, L + 1)
                nc.vector.tensor_tensor(f1_lo, raw_f, f1_hi.bitcast(F32), ALU.subtract).then_inc(f1_lo_s, 1)
                rows_lo(c, 2, groups + 1, FG, 0)
                par_ready(dve, L, 2)

                def step(i, s, first, last_body):
                    g = i * 2 + s
                    u = groups * FC + (i * (2 * FC) + s * FC)
                    if exists(2, s, first, last_body, 0):
                        if not (last_body and s == 1):
                            rows_norm(c, groups + (g + 1), FG, i * (2 * FG) + (s + 1) * FG)
                        for ch in range(FC):
                            dve.wait_ge(c["a"], u + (ch + 1))
                            dve.wait_ge(c["gelu"], u + (ch + 1))
                            if ch == 0 and not (first and s < 2):
                                dve.wait_ge(c["y"], batches + (g - 1) * FG)
                            nc.vector.scalar_tensor_tensor(out=hid[:, s % 2, ch, :], in0=it_ps[ch % 2][:],
                                                           scalar=fb[:, ch:ch + 1], in1=gel[:, ch, :],
                                                           op0=ALU.add, op1=ALU.mult).then_inc(c["hid"], 1)
                        if not (last_body and s == 1):
                            rows_lo(c, 2, groups + (g + 2), FG, 1 - s)
                    if exists(2, s, first, last_body, 1):
                        for b in range(FG):
                            bl = i * (2 * FG) + (s - 1) * FG + b
                            residual(c, 2, (ot_ps, tr_ps)[b % 2][:, 0:P], batches + bl, bl)

                bodies(dve, FNI, 2, 1, step)
                dve.wait_ge(c["xstat"], batches + B)

            for ph in (*PHASES,):
                S[ph.name]["xstat"] = sem(f"{ph.name}_xstat")
            FS["xstat"] = sem("ff_xstat")
            for L in range(LAYERS):
                for n, ph in enumerate(PHASES):
                    attention(n, ph, L)
                feed_forward(L)


def kernel(**inputs):
    import numpy as np
    import concourse.bacc as bacc
    from concourse.bass_utils import run_bass_kernel_spmd as run

    def a(name):
        return np.asarray(inputs[name])

    L0, L1 = "L0_xattn_", "L1_xattn_"

    def both(f0, f1=None):
        return np.ascontiguousarray(np.stack([f0(L0), (f1 or f0)(L1)]))

    lay = {
        "x": np.ascontiguousarray(a("x")),
        "ctx_t": np.ascontiguousarray(a("ctx_768").transpose(2, 0, 1)),
        "wq_t": both(lambda p: np.stack([a(p + "Wq1").T, a(p + "Wq2").T])),
        "wk_t": both(lambda p: a(p + "Wk1").T),
        "wv": both(lambda p: a(p + "Wv1")),
        "wo": both(lambda p: np.stack([a(p + "Wo1"), a(p + "Wo2")])),
        "bo": both(lambda p: np.stack([a(p + "bo1"), a(p + "bo2"), a(p + "bff2")]),
                   lambda p: np.stack([a(p + "bo1"), a(p + "bo2"), a(p + "bf")])),
        "wk2_t": both(lambda p: a(p + "Wk2").T),
        "wv2": both(lambda p: a(p + "Wv2")),
        "ln_g": both(lambda p: np.stack([np.stack([a(f"{p}ln{n}_g"), a(f"{p}ln{n}_b")], -1) for n in (1, 2, 3)]),
                     lambda p: np.stack([np.stack([a(f"{p}g{n}"), a(f"{p}b{n}")], -1) for n in (1, 2, 3)])),
        "ln_b": np.zeros((1, 2), np.float32),
        "w1": both(lambda p: a(p + "Wff1"), lambda p: a(p + "Wp")),
        "b1": both(lambda p: a(p + "bff1").reshape(-1, P).T, lambda p: a(p + "bp").reshape(-1, P).T),
        "w2": both(lambda p: a(p + "Wff2"), lambda p: a(p + "Wf")),
    }
    del lay["ln_b"]
    nc = bacc.Bacc("TRN2", target_bir_lowering=False, num_devices=1)
    aps = {k: nc.dram_tensor("in_" + k, v.shape, mybir.dt.from_np(v.dtype), kind="ExternalInput").ap() for k, v in lay.items()}
    y = nc.dram_tensor("out_y", lay["x"].shape, F32, kind="ExternalOutput").ap()
    block_kernel(nc, aps["x"], aps["ctx_t"], aps["wq_t"], aps["wk_t"], aps["wv"], aps["wo"], aps["bo"],
                 aps["wk2_t"], aps["wv2"], aps["ln_g"], None, aps["w1"], aps["b1"], aps["w2"], y)
    r = run(nc, [{"in_" + k: v for k, v in lay.items()}], core_ids=[0])
    return r.results[0]["out_y"]
```

```python
from contextlib import ExitStack

import concourse.bass as bass
from concourse import mybir

F32 = mybir.dt.float32
F32R = mybir.dt.float32r
I32 = mybir.dt.int32
ALU = mybir.AluOpType
ACT = mybir.ActivationFunctionType
AX = mybir.AxisListType

P = 128
HEADS, DH = 16, 64
INNER = HEADS * DH
CHUNKS = INNER // P
HG = 4
UPB = HEADS // HG
LAYERS = 2
EPS = 1e-5
PS_BANK = 512
VRING = 4
PRING = 4
EXP_LAG, T_LAG, PV_LAG, Y_LAG = 1, 3, 4, 5
OPEN_AT = 5
OPEN_ITEMS = 5
OPEN_PARTS = 9
RSQRT_BITS = 0x5f3759df
NEWTON = 3
STAGES = 6 + 3 * NEWTON
STORES = 8
IBANKS = 3


class Attention:

    def __init__(self, name, batches, group, keys, kv_dim, heads_per_item, w_steps):
        self.name, self.B, self.G, self.J, self.E = name, batches, group, keys, kv_dim
        self.JP = keys + keys % 2
        self.GJ = group * self.JP
        self.HI = heads_per_item
        self.U = UPB * group
        self.UB = 2 * self.U
        self.NI = batches // (2 * group)
        self.groups = batches // group
        self.units = UPB * batches
        self.w_per_group = HEADS // heads_per_item
        self.plan = []
        rest = list(range(self.w_per_group))
        for s in range(self.U):
            here = [("v", s // UPB, s % UPB)] if s % UPB < 2 else []
            here += [("w", rest.pop(0)) for _ in range(w_steps[s])]
            self.plan.append(here)
        assert not rest
        self.v_ahead = 1
        self.items_per_body = 2 * (self.w_per_group + 2 * group)
        self.items_prologue = self.w_per_group + 2 * self.v_ahead
        self.items = self.w_per_group * self.groups + 2 * batches

    def body(self, last):
        out, n, w, v = [[] for _ in range(self.UB)], 0, 0, 0
        for s in range(self.UB):
            for it in self.plan[s % self.U]:
                if it[0] == "w":
                    if last and s >= self.U:
                        continue
                    out[s].append(("w", it[1], 1 - s // self.U, n, w))
                    w += 1
                else:
                    b = s // UPB + self.v_ahead
                    if last and b >= 2 * self.G:
                        continue
                    out[s].append(("v", b, it[2], n, v))
                    v += 1
                n += 1
        return out

    def v_count(self, i, b, first, last):
        if b < self.v_ahead:
            if first:
                return self.w_per_group + 2 * b + 2
            plan, off = self.body(False), b + 2 * self.G
            n = next(it[3] for s in plan for it in s if it[:3] == ("v", off, 1)) - self.items_per_body
        else:
            n = next(it[3] for s in self.body(last) for it in s if it[:3] == ("v", b, 1))
        return i * self.items_per_body + (self.items_prologue + n + 1)

    def w_count(self, i, s, first, last):
        g, item = s // self.U, (HG * (s % self.U) + HG - 1) // self.HI
        if g == 0:
            if first:
                return item + 1
            n = next(it[3] for st in self.body(False)[self.U:] for it in st if it[:2] == ("w", item)) - self.items_per_body
        else:
            n = next(it[3] for st in self.body(last)[:self.U] for it in st if it[:2] == ("w", item))
        return i * self.items_per_body + (self.items_prologue + n + 1)

    def prologue_part(self, part):
        if part < OPEN_ITEMS:
            return []
        its, parts, p = self.prologue(), OPEN_PARTS - OPEN_ITEMS, part - OPEN_ITEMS
        return its[len(its) * p // parts:len(its) * (p + 1) // parts]

    def prologue(self):
        out = [("w", j, 0, j, j) for j in range(self.w_per_group)]
        for b in range(self.v_ahead):
            for half in range(2):
                v = 2 * b + half
                out.append(("v", b, half, self.w_per_group + v, v))
        return out


def block_kernel(nc, x_in, ctx_t, wq_t, wk_t, wv, wo, bo, wk2_t, wv2, ln_gb, w1, b1, w2, out):
    B = x_in.shape[0]
    J2 = ctx_t.shape[2]
    E2 = ctx_t.shape[0]
    FF = w1.shape[2] // 2
    FC = FF // P
    FG = 4
    FN = FG * P
    FNI = B // (2 * FG)
    assert FC == FG
    SELF = Attention("self", B, 2, P, P, 2, [0, 0, 1, 2, 1, 1, 1, 2])
    CROSS = Attention("ctx", B, 4, J2, E2, 1, [0, 0, 1, 2, 1, 1, 1, 2] + 2 * [0, 1, 1, 2])
    PHASES = (SELF, CROSS)
    GMAX = 4
    X_PARTS = (0, B // 8, B // 4, B // 2, 3 * B // 4, B)
    assert X_PARTS[1] >= 4 * SELF.G

    ctx = ExitStack()
    with ctx:
        def sb(name, shape, dt=F32):
            return ctx.enter_context(nc.sbuf_tensor(name, shape, dt))

        def sem(name):
            return ctx.enter_context(nc.semaphore(name))

        x = sb("x", [P, B, P])
        stats = sb("stats", [P, B, 6])
        rstd = sb("rstd", [P, B])
        nmr = sb("nmr", [P, B])
        ident = sb("ident", [P, P])
        xn = sb("xn", [P, GMAX, P])
        xfull = sb("xfull", [P, GMAX * P])
        xt_hi = sb("xt_hi", [P, 2, GMAX * P], F32R)
        xt_lo = sb("xt_lo", [P, 2, GMAX * P], F32R)
        c_hi = sb("c_hi", [E2, 2, CROSS.GJ], F32R)
        c_lo = sb("c_lo", [E2, 2, CROSS.GJ], F32R)
        a_hi = sb("a_hi", [P, HEADS, P], F32R)
        a_lo = sb("a_lo", [P, HEADS, P], F32R)
        wv_hi = sb("wv_hi", [P, INNER], F32R)
        wv_lo = sb("wv_lo", [P, INNER], F32R)
        wo_sb = sb("wo_sb", [P, CHUNKS, P])
        bo_bc = sb("bo_bc", [P, P])
        gb = sb("gb", [P, 3, 2])
        raw = sb("raw", [P, 2, INNER])
        w_hi = sb("w_hi", [P, 2, HEADS * CROSS.GJ], F32R)
        w_lo = sb("w_lo", [P, 2, HEADS * CROSS.GJ], F32R)
        v_sb = sb("v_sb", [P, VRING, INNER])
        probs = sb("probs", [P, PRING, HG, P])
        nmax = sb("nmax", [P, PRING, HG])
        rsum = sb("rsum", [P, PRING, HG])
        rrec = sb("rrec", [P, PRING, HG])
        pt = sb("pt", [P, PRING, HG * P])
        ot = sb("ot", [P, 2, CHUNKS // 2, P])
        ytmp = sb("ytmp", [P, P])
        fb = sb("fb", [P, 2 * FC])
        raw_q, raw_k = raw[:, 0, :], raw[:, 1, :]
        raw_v = v_sb[:, 0, :]
        f2_sb = wo_sb[:, 0:FC, :]
        craw = raw[0:E2, 1, 0:CROSS.GJ].rearrange("p (b j) -> p b j", b=GMAX)
        f1_hi = a_hi[:, 0:2 * FC, :].rearrange("p c n -> p (c n)")
        f1_lo = a_lo[:, 0:2 * FC, :].rearrange("p c n -> p (c n)")
        gel = probs[:].rearrange("p a b c -> p a (b c)")
        raw_f = raw[:, 0, :]
        hid = v_sb[:].rearrange("p (a b) (c n) -> p a (b c) n", a=2, n=FN)

        def bank(name):
            return ctx.enter_context(nc.psum_tensor(name, [P, PS_BANK], F32))
        sc_ps = [bank(f"sc_ps{i}") for i in range(2)]
        tr_ps = bank("tr_ps")
        it_ps = [bank(f"it_ps{i}") for i in range(IBANKS)]
        ot_ps = bank("ot_ps")
        y_ps = bank("y_ps")

        x_loaded = [sem(f"x_loaded{i}") for i in range(len(X_PARTS) - 1)]
        x_stats = sem("x_stats")
        ident_zero, ident_ready = sem("ident_zero"), sem("ident_ready")
        moments = sem("moments")
        raw_in = sem("raw_in")
        raw_v_in = sem("raw_v_in")
        ln_in = [sem(f"ln_in{n}") for n in range(3)]
        par_in = sem("par_in")
        wprod_ps, wprod_hi, wprod_lo = sem("wprod_ps"), sem("wprod_hi"), sem("wprod_lo")
        wv_hi_s, wv_lo_s = sem("wv_hi_s"), sem("wv_lo_s")
        f1_hi_s, f1_lo_s = sem("f1_hi_s"), sem("f1_lo_s")
        out_done = sem("out_done")
        S = {}
        for ph in PHASES:
            S[ph.name] = {k: sem(f"{ph.name}_{k}") for k in (
                "scores", "nmax", "exps", "recips", "normed", "turned", "pt", "pv", "ot", "y", "ysum",
                "resid", "xstat", "item", "whi", "evac", "xn", "xnT", "xhi", "xfull", "xlo", "craw", "chi", "clo")}
        FS = {k: sem(f"ff_{k}") for k in ("xn", "xnT", "xhi", "xfull", "xlo", "gate", "a", "gelu", "hid",
                                          "y", "ysum", "resid", "xstat")}

        RAW_DMAS = (2, 2, 1)
        LN_DMAS = (1, 1, 2)

        def following(L, n):
            return (L, n + 1) if n < 2 else (L + 1, 0) if L + 1 < LAYERS else None

        block = ctx.enter_context(nc.Block())

        def ysum_of_before(L, n):
            return (FS["ysum"], L * B) if n == 0 else (S[PHASES[n - 1].name]["ysum"], (L + 1) * B)

        def stats_part(L, n, half):
            cut = X_PARTS[1] if (L, n) == (0, 0) else 3 * B // 4
            return slice(0, cut) if half == 0 else slice(cut, B), ((L * 3 + n) * 2 + half) * STAGES

        def open_next(opening, L, n, s, ph):
            part = s - (ph.UB - OPEN_AT)
            if 0 <= part < OPEN_PARTS:
                opening(*following(L, n), part)

        def open_next_ff(opening, L, b):
            if following(L, 2):
                for part in range(b, b + 1 if b + 1 < FG else OPEN_PARTS):
                    opening(*following(L, 2), part)

        def bodies(eng, NI, steps, lag, step):
            for s in range(steps):
                step(0, s, True, False)
            with eng.Fori(1, NI - 1) as i:
                for s in range(steps):
                    step(i, s, False, False)
            for s in range(steps + lag):
                step(NI - 1, s, False, True)

        def exists(ph_steps, s, first, last, lag):
            return not (first and s < lag) and not (last and s - lag >= ph_steps)

        @block.sync
        def _(sp):
            def load_x(c):
                rows = slice(X_PARTS[c], X_PARTS[c + 1])
                sp.dma_start(x[:, rows, :], x_in[rows].rearrange("b t d -> t b d")).then_inc(x_loaded[c], 16)

            load_x(0)
            for L in range(LAYERS):
                for n in range(3):
                    prev = L * 3 + n
                    if prev and n != 0:
                        sp.wait_ge(wprod_ps, L * 4 + 2 * n)
                    elif prev:
                        sp.wait_ge(f1_lo_s, L)
                    if n < 2:
                        ph, kt, vv = (SELF, wk_t, wv) if n == 0 else (CROSS, wk2_t, wv2)
                        E = ph.E
                        sp.dma_start(raw_q.rearrange("p (c n) -> p c n", c=CHUNKS),
                                     wq_t[L, n].rearrange("(c p) n -> p c n", p=P)).then_inc(raw_in, 16)
                        sp.dma_start(raw_k[:, 0:CHUNKS * E].rearrange("p (c n) -> p c n", c=CHUNKS),
                                     kt[L].rearrange("(c p) n -> p c n", p=P)).then_inc(raw_in, 16)
                    else:
                        sp.dma_start(raw_f, w1[L]).then_inc(raw_in, 16)
                        sp.dma_start(fb[:], b1[L]).then_inc(ln_in[n], 16)
                    sp.dma_start(gb[:, n, :], ln_gb[L, n]).then_inc(ln_in[n], 16)
                    if n < 2:
                        if n == 1:
                            sp.wait_ge(S["self"]["pv"], ((L + 1) * SELF.units - (VRING - 1) * UPB) // 2)
                        elif prev:
                            sp.wait_ge(FS["y"], L * B - FG)
                        sp.dma_start(raw_v[0:E, :], vv[L]).then_inc(raw_v_in, 16)
                    if not prev:
                        for c in range(1, len(x_loaded)):
                            load_x(c)
                    if n == 1:
                        c = S["ctx"]
                        sp.wait_ge(wprod_ps, L * 4 + 4)
                        sp.dma_start(craw[:, :, 0:J2], ctx_t[:, 0:CROSS.G, :]).then_inc(c["craw"], 16)
                        sp.wait_ge(c["clo"], L * CROSS.groups + 1)
                        sp.dma_start(craw[:, :, 0:J2], ctx_t[:, CROSS.G:2 * CROSS.G, :]).then_inc(c["craw"], 16)
                    if prev:
                        sp.wait_ge(*((FS["y"], L * B) if n == 0 else (S[PHASES[n - 1].name]["y"], (L + 1) * B * 2)))
                    if n < 2:
                        sp.dma_start(wo_sb[:], wo[L, n].rearrange("(c p) n -> p c n", p=P)).then_inc(par_in, 16)
                    else:
                        sp.dma_start(f2_sb, w2[L].rearrange("(c p) n -> p c n", p=P)).then_inc(par_in, 16)
                    if prev:
                        sp.wait_ge(*ysum_of_before(L, n))
                    sp.dma_start(bo_bc[:], bo[L, n:n + 1, :].to_broadcast([P, P])).then_inc(par_in, 16)
                    if n == 1:
                        with sp.Fori(2, CROSS.groups) as g:
                            sp.wait_ge(c["clo"], L * CROSS.groups + g)
                            sp.dma_start(craw[:, :, 0:J2], ctx_t[:, bass.ts(g, CROSS.G), :]).then_inc(c["craw"], 16)
            for c in range(STORES):
                rows = slice(c * B // STORES, (c + 1) * B // STORES)
                sp.wait_ge(FS["resid"], (LAYERS - 1) * B + rows.stop)
                sp.dma_start(out[rows].rearrange("b t d -> t b d"), x[:, rows, :]).then_inc(out_done, 16)
            sp.wait_ge(out_done, 16 * STORES)

        def raw_ready(eng, L, n):
            eng.wait_ge(raw_in, 16 * (L * sum(RAW_DMAS) + sum(RAW_DMAS[:n + 1])))

        def ln_ready(eng, L, n):
            eng.wait_ge(ln_in[n], 16 * (L + 1) * LN_DMAS[n])

        def par_ready(eng, L, n):
            eng.wait_ge(par_in, 16 * 2 * (L * 3 + n + 1))

        @block.gpsimd
        def _(pool):
            nc.gpsimd.memset(ident[:], 0.0).then_inc(ident_zero, 1)
            pool.wait_ge(ident_zero, 1)
            nc.gpsimd.affine_select(out=ident[:], in_=ident[:], compare_op=ALU.not_equal, fill=1.0,
                                    base=0, pattern=[[-1, P]], channel_multiplier=1).then_inc(ident_ready, 1)

            def attention(n, ph, L):
                c = S[ph.name]
                base = L * ph.units

                def step(i, s, first, last):
                    if not exists(ph.UB, s, first, last, 0):
                        return
                    k = base + (i * ph.UB + s)
                    pr = probs[:, s % PRING, :, 0:ph.J]
                    pool.wait_ge(c["recips"], k + 1)
                    nc.gpsimd.tensor_tensor(pr, pr, rrec[:, s % PRING, :].unsqueeze(2).to_broadcast([P, HG, ph.J]),
                                            ALU.mult).then_inc(c["normed"], 1)

                bodies(pool, ph.NI, ph.UB, 0, step)

            for L in range(LAYERS):
                for n, ph in enumerate(PHASES):
                    attention(n, ph, L)

        @block.tensor
        def _(pe):
            def three(out_, l_hi, l_lo, r_hi, r_lo):
                nc.tensor.matmul(out_, l_hi, r_hi, start=True, stop=False)
                nc.tensor.matmul(out_, l_hi, r_lo, start=False, stop=False)
                return nc.tensor.matmul(out_, l_lo, r_hi, start=False, stop=True)

            def turn_rows(c, dst, g_count, G):
                pe.wait_ge(c["xn"], g_count)
                for b in range(G):
                    last = nc.tensor.transpose(dst[:, b * P:(b + 1) * P], xn[:, b, :], ident[:])
                last.then_inc(c["xnT"], 1)

            def kv(n, ph, par, b=None):
                hi, lo = (xt_hi, xt_lo) if n == 0 else (c_hi, c_lo)
                if b is None:
                    return hi[0:ph.E, par, 0:ph.GJ], lo[0:ph.E, par, 0:ph.GJ]
                return hi[0:ph.E, par, b * ph.JP:b * ph.JP + ph.J], lo[0:ph.E, par, b * ph.JP:b * ph.JP + ph.J]

            def kv_ready(n, ph, g):
                pe.wait_ge(S[ph.name]["xlo"], g)
                if n == 1:
                    pe.wait_ge(S[ph.name]["clo"], g)

            def item(n, ph, it, base, off):
                kind, a, z, m, q = it
                c, E = S[ph.name], ph.E
                dst = it_ps[(m + off) % IBANKS]
                if m + off >= IBANKS:
                    pe.wait_ge(c["evac"], base + (m + 1 - IBANKS))
                if kind == "w":
                    hi, lo = kv(n, ph, z)
                    for t in range(ph.HI):
                        h = a * ph.HI + t
                        last = three(dst[:, t * ph.GJ:(t + 1) * ph.GJ], a_hi[0:E, h, :], a_lo[0:E, h, :], hi, lo)
                else:
                    hi, lo = kv(n, ph, (a // ph.G) % 2, a % ph.G)
                    cols = slice(z * PS_BANK, (z + 1) * PS_BANK)
                    last = three(dst[0:ph.J, :], hi, lo, wv_hi[0:E, cols], wv_lo[0:E, cols])
                last.then_inc(c["item"], 1)

            def head_products(L, n, r):
                E = PHASES[n].E
                for j in range(4):
                    for odd in range(2):
                        h = 8 * r + 2 * j + odd
                        rows = slice(DH * odd, DH * odd + DH)
                        last = nc.tensor.matmul(it_ps[odd][0:E, j * P:(j + 1) * P],
                                                raw_k[rows, (h // 2) * E:(h // 2 + 1) * E],
                                                raw_q[rows, (h // 2) * P:(h // 2 + 1) * P], start=True, stop=True)
                last.then_inc(wprod_ps, 1)

            def opening(L, n, part):
                if part == 0:
                    if n == 0 and L:
                        pe.wait_ge(FS["hid"], L * (B // FG) * FC)
                    if n:
                        before = PHASES[n - 1]
                        pe.wait_ge(S[before.name]["evac"], (L + 1) * before.items)
                    if n < 2:
                        raw_ready(pe, L, n)
                        head_products(L, n, 0)
                if part == 1:
                    c, G, groups = (S[PHASES[n].name], PHASES[n].G, L * PHASES[n].groups) if n < 2 else (FS, FG, L * (B // FG))
                    turn_rows(c, it_ps[2], groups + 1, G)
                if part == 2 and n < 2:
                    pe.wait_ge(wprod_lo, L * 8 + (4 * n + 2))
                    head_products(L, n, 1)
                if n < 2:
                    ph = PHASES[n]
                    if part == OPEN_ITEMS:
                        pe.wait_ge(wprod_lo, L * 8 + (4 * n + 4))
                        pe.wait_ge(wv_lo_s, L * 2 + (n + 1))
                        kv_ready(n, ph, L * ph.groups + 1)
                    for it in ph.prologue_part(part):
                        item(n, ph, it, L * ph.items, 0)

            def attention(n, ph, L):
                c = S[ph.name]
                E, J, JP = ph.E, ph.J, ph.JP
                units, items, groups, batches = L * ph.units, L * ph.items, L * ph.groups, L * ph.B
                plans = {False: ph.body(False), True: ph.body(True)}

                def step(i, s, first, last_body):
                    k = units + (i * ph.UB + s)
                    if exists(ph.UB, s, first, last_body, 0):
                        g, gs, b = s // ph.U, s % ph.U, s // UPB
                        if gs < UPB:
                            pe.wait_ge(c["evac"], items + ph.w_count(i, s, first, last_body))
                        if not (first and s < 2):
                            pe.wait_ge(c["exps"], k - 1)
                        bank_ = sc_ps[s % 2][:, 0:HG * JP]
                        h0 = HG * (s % UPB)
                        bg = b % ph.G
                        cols = slice(bg * P, (bg + 1) * P)

                        def w(t):
                            return t[:, g % 2, 0:HEADS * ph.GJ].rearrange("p (h j) -> p h j", h=HEADS)[
                                :, h0:h0 + HG, bg * JP:(bg + 1) * JP]
                        three(bank_, xt_hi[:, g % 2, cols], xt_lo[:, g % 2, cols], w(w_hi), w(w_lo)).then_inc(c["scores"], 1)
                        its = plans[last_body][s]
                        ib = items + (i * ph.items_per_body + ph.items_prologue)
                        more = not (last_body and g == 1)
                        if gs == 2 and more:
                            kv_ready(n, ph, groups + (i * 2 + g + 2))
                        for it in its[:1]:
                            item(n, ph, it, ib, ph.items_prologue)
                    else:
                        its = []
                    def turn_probs():
                        if exists(ph.UB, s, first, last_body, T_LAG):
                            u = s - T_LAG
                            pe.wait_ge(c["normed"], k - T_LAG + 1)
                            if not (first and u < 1):
                                pe.wait_ge(c["pt"], k - T_LAG)
                            for t in range(HG):
                                last = nc.tensor.transpose(tr_ps[0:J, t * P:(t + 1) * P],
                                                           probs[:, u % PRING, t, 0:J], ident[:])
                            last.then_inc(c["turned"], 1)

                    rows = s < ph.UB and gs == 0 and more
                    if rows:
                        if not (first and s < T_LAG + 1):
                            pe.wait_ge(c["pt"], k - T_LAG)
                        elif n == 0 and L:
                            pe.wait_ge(*ysum_of_before(L, n))
                        turn_rows(c, tr_ps, groups + (i * 2 + g + 2), ph.G)
                    else:
                        turn_probs()
                    if exists(ph.UB, s, first, last_body, PV_LAG) and (s - PV_LAG) % 2:
                        b = (s - PV_LAG) // UPB
                        pair = units // 2 + (i * (ph.UB // 2) + (s - PV_LAG) // 2)
                        pe.wait_ge(c["pt"], k - PV_LAG + 1)
                        if not (first and s - PV_LAG == 1):
                            pe.wait_ge(c["ot"], pair)
                        if (s - PV_LAG) % UPB == 1:
                            pe.wait_ge(c["evac"], items + ph.v_count(i, b, first, last_body))
                        for u in (s - PV_LAG - 1, s - PV_LAG):
                            h0 = HG * (u % UPB)
                            for t in range(HG):
                                col = (u % 2 * HG + t) // 2 * P
                                last = nc.tensor.matmul(ot_ps[DH * (t % 2):DH * (t % 2) + DH, col:col + P],
                                                        v_sb[0:J, b % VRING, (h0 + t) * DH:(h0 + t + 1) * DH],
                                                        pt[0:J, u % PRING, t * P:(t + 1) * P], start=True, stop=True)
                        last.then_inc(c["pv"], 1)
                    for it in its[1:]:
                        item(n, ph, it, ib, ph.items_prologue)
                    if exists(ph.UB, s, first, last_body, Y_LAG) and (s - Y_LAG) % 2:
                        b, half = (s - Y_LAG) // UPB, (s - Y_LAG) % UPB // 2
                        pe.wait_ge(c["ot"], units // 2 + (i * (ph.UB // 2) + (s - Y_LAG) // 2 + 1))
                        if half == 0 and first and b == 0:
                            par_ready(pe, L, n)
                            if n:
                                pe.wait_ge(*ysum_of_before(L, n))
                        elif half == 0:
                            pe.wait_ge(c["ysum"], batches + (i * (2 * ph.G) + b))
                        for ch in range(half * CHUNKS // 2, (half + 1) * CHUNKS // 2):
                            last = nc.tensor.matmul(y_ps[:, 0:P], ot[:, half, ch % (CHUNKS // 2), :], wo_sb[:, ch, :],
                                                    start=(ch == 0), stop=(ch == CHUNKS - 1))
                        last.then_inc(c["y"], 1)
                    if rows:
                        pe.wait_ge(c["xfull"], groups + (i * 2 + g + 2))
                        turn_probs()
                    if last_body:
                        open_next(opening, L, n, s, ph)

                bodies(pe, ph.NI, ph.UB, Y_LAG, step)

            def feed_forward(L):
                c = FS
                groups, batches = L * (B // FG), L * B
                pe.wait_ge(f1_lo_s, L + 1)
                pe.wait_ge(*ysum_of_before(L, 2))

                def step(i, s, first, last_body):
                    g = i * 2 + s
                    u = groups * FC + (i * (2 * FC) + s * FC)
                    hi, lo = xt_hi[:, s % 2, :], xt_lo[:, s % 2, :]
                    for ch in range(FC):
                        if exists(2, s, first, last_body, 0):
                            if ch == 0:
                                pe.wait_ge(c["xlo"], groups + (g + 1))
                            ga, aa = sc_ps[ch % 2], it_ps[ch % 2]
                            if not (first and s == 0 and ch < 2):
                                pe.wait_ge(c["gelu"], u + (ch - 1))
                            cols = slice(FF + ch * P, FF + (ch + 1) * P)
                            three(ga[:], f1_hi[:, cols], f1_lo[:, cols], hi, lo).then_inc(c["gate"], 1)
                            if not (first and s == 0 and ch < 2):
                                pe.wait_ge(c["hid"], u + (ch - 1))
                            cols = slice(ch * P, (ch + 1) * P)
                            three(aa[:], f1_hi[:, cols], f1_lo[:, cols], hi, lo).then_inc(c["a"], 1)
                            if ch == 1 and not (last_body and s == 1):
                                turn_rows(c, y_ps, groups + (g + 2), FG)
                        if exists(2, s, first, last_body, 1):
                            bb = batches + ((g - 1) * FG + ch)
                            if ch == 0:
                                pe.wait_ge(c["hid"], u)
                            if ch == 0 and first and s == 1:
                                par_ready(pe, L, 2)
                            if not (first and s == 1 and ch < 2):
                                pe.wait_ge(c["ysum"], bb - 1)
                            for hc in range(FC):
                                last = nc.tensor.matmul((ot_ps, tr_ps)[ch % 2][:, 0:P],
                                                        hid[:, (s - 1) % 2, hc, ch * P:(ch + 1) * P],
                                                        f2_sb[:, hc, :], start=(hc == 0), stop=(hc == FC - 1))
                            last.then_inc(c["y"], 1)
                        if s == 2:
                            open_next_ff(opening, L, ch)

                bodies(pe, FNI, 2, 1, step)

            pe.wait_ge(ident_ready, 1)
            for part in range(OPEN_PARTS):
                opening(0, 0, part)
            for L in range(LAYERS):
                for n, ph in enumerate(PHASES):
                    attention(n, ph, L)
                feed_forward(L)

        @block.scalar
        def _(act):
            def rows_hi(c, count, G, par):
                act.wait_ge(c["xfull"], count)
                nc.scalar.copy(xt_hi[:, par, 0:G * P], xfull[:, 0:G * P]).then_inc(c["xhi"], 1)

            def context_hi(n, ph, g, par):
                c = S[ph.name]
                if n == 1:
                    act.wait_ge(c["craw"], 16 * g)
                    nc.scalar.copy(c_hi[:, par, :], craw[:].rearrange("p b j -> p (b j)")).then_inc(c["chi"], 1)

            def item_hi(ph, it, base, off):
                kind, a, z, m, q = it
                c = S[ph.name]
                if kind == "w":
                    act.wait_ge(c["item"], base + (m + 1))
                    nc.scalar.copy(w_hi[:, z, a * ph.HI * ph.GJ:(a + 1) * ph.HI * ph.GJ],
                                   it_ps[(m + off) % IBANKS][:, 0:ph.HI * ph.GJ]).then_inc(c["whi"], 1)

            def opening(L, n, part):
                if part == 0:
                    if n:
                        act.wait_ge(S[PHASES[n - 1].name]["item"], (L + 1) * PHASES[n - 1].items)
                    elif L:
                        act.wait_ge(FS["a"], L * (B // FG) * FC)
                if part == 0 and n == 2:
                    raw_ready(act, L, n)
                    nc.scalar.copy(f1_hi, raw_f).then_inc(f1_hi_s, 1)
                if part in (0, 2) and n < 2:
                    r, E = part // 2, PHASES[n].E
                    act.wait_ge(wprod_ps, L * 4 + (2 * n + r + 1))
                    for odd in range(2):
                        nc.scalar.activation(a_hi[0:E, 8 * r + odd:8 * r + 8:2, :],
                                             it_ps[odd][0:E, :].rearrange("p (h n) -> p h n", h=4), ACT.Copy,
                                             scale=DH ** -0.5).then_inc(wprod_hi, 1)
                if part == 1:
                    if n == 2:
                        rows_hi(FS, L * (B // FG) + 1, FG, 0)
                    else:
                        rows_hi(S[PHASES[n].name], L * PHASES[n].groups + 1, PHASES[n].G, 0)
                if n < 2:
                    ph = PHASES[n]
                    if part == 3:
                        act.wait_ge(raw_v_in, 16 * (2 * L + n + 1))
                        nc.scalar.copy(wv_hi[0:ph.E, :], raw_v[0:ph.E, :]).then_inc(wv_hi_s, 1)
                    if part == 4:
                        context_hi(n, ph, L * ph.groups + 1, 0)
                    for it in ph.prologue_part(part):
                        item_hi(ph, it, L * ph.items, 0)
                    if part == OPEN_PARTS - 1:
                        context_hi(n, ph, L * ph.groups + 2, 1)

            def attention(n, ph, L):
                c = S[ph.name]
                J, JP = ph.J, ph.JP
                units, items, groups = L * ph.units, L * ph.items, L * ph.groups
                if n == 0 and L:
                    act.wait_ge(FS["hid"], L * (B // FG) * FC)
                plans = {False: ph.body(False), True: ph.body(True)}

                def step(i, s, first, last_body):
                    k = units + (i * ph.UB + s)
                    its = []
                    if exists(ph.UB, s, first, last_body, 0):
                        g, gs = s // ph.U, s % ph.U
                        ib = items + (i * ph.items_per_body + ph.items_prologue)
                        its = plans[last_body][s]
                        more = not (last_body and g == 1)
                    if exists(ph.UB, s, first, last_body, EXP_LAG):
                        u = s - EXP_LAG
                        act.wait_ge(c["nmax"], k - EXP_LAG + 1)
                        if not (first and u < PRING):
                            act.wait_ge(c["turned"], k - EXP_LAG - PRING + 1)
                        for t in range(HG):
                            last = nc.scalar.activation(
                                probs[:, u % PRING, t, 0:J], sc_ps[u % 2][:, t * JP:t * JP + J], ACT.Exp,
                                bias=nmax[:, u % PRING, t:t + 1], scale=1.0,
                                accum_out=rsum[:, u % PRING, t:t + 1])
                        last.then_inc(c["exps"], 1)
                    for it in its[:1]:
                        item_hi(ph, it, ib, ph.items_prologue)
                    if s < ph.UB and gs == 0 and more:
                        rows_hi(c, groups + (i * 2 + g + 2), ph.G, 1 - g)
                    if exists(ph.UB, s, first, last_body, T_LAG):
                        u = s - T_LAG
                        act.wait_ge(c["turned"], k - T_LAG + 1)
                        if first and u == 0 and n:
                            act.wait_ge(S[PHASES[n - 1].name]["pv"], (L + 1) * PHASES[n - 1].units // 2)
                        if not (first and u < PRING):
                            act.wait_ge(c["pv"], units // 2 + (i * (ph.UB // 2) + u // 2 - 1))
                        nc.scalar.copy(pt[0:J, u % PRING, :], tr_ps[0:J, :]).then_inc(c["pt"], 1)
                    for it in its[1:]:
                        item_hi(ph, it, ib, ph.items_prologue)
                    if s < ph.UB and gs == ph.U - 2 and not last_body:
                        context_hi(n, ph, groups + (i * 2 + g + 3), g)
                    if last_body:
                        open_next(opening, L, n, s, ph)

                bodies(act, ph.NI, ph.UB, Y_LAG, step)

            def feed_forward(L):
                c = FS
                groups = L * (B // FG)
                def step(i, s, first, last_body):
                    if s == 2:
                        for b in range(FG):
                            open_next_ff(opening, L, b)
                        return
                    u = groups * FC + (i * (2 * FC) + s * FC)
                    for ch in range(FC):
                        act.wait_ge(c["gate"], u + (ch + 1))
                        if not (first and s == 0):
                            act.wait_ge(c["hid"], u + (ch + 1 - FC))
                        nc.scalar.activation(gel[:, ch, :], sc_ps[ch % 2][:], ACT.Gelu,
                                             bias=fb[:, FC + ch:FC + ch + 1], scale=1.0).then_inc(c["gelu"], 1)
                        if ch == 2 and not (last_body and s == 1):
                            rows_hi(c, groups + (i * 2 + s + 2), FG, 1 - s)

                bodies(act, FNI, 2, 1, step)

            for part in range(OPEN_PARTS):
                opening(0, 0, part)
            for L in range(LAYERS):
                for n, ph in enumerate(PHASES):
                    attention(n, ph, L)
                feed_forward(L)

        @block.vector
        def _(dve):
            STAT_STEPS = 8
            STAT_ROWS = (B - X_PARTS[1]) // STAT_STEPS

            def rows_stats(first, last):
                for b in range(first, last):
                    if b in X_PARTS or b == first:
                        dve.wait_ge(x_loaded[sum(b >= p for p in X_PARTS) - 1], 16)
                    ins = nc.vector.bn_stats(stats[:, b, :], x[:, b, :])
                ins.then_inc(x_stats, 1)

            def statistics(L, n, half, stage):
                cols, base = stats_part(L, n, half)
                me, qe, mo, qo = (stats[:, cols, j] for j in (1, 2, 4, 5))
                total, diff, q, var, t = (stats[:, cols, j] for j in (0, 3, 5, 4, 1))
                r = rstd[:, cols]
                if stage:
                    dve.wait_ge(moments, base + stage)
                elif (L, n) == (0, 0):
                    dve.wait_ge(x_stats, 1 + STAT_STEPS if half else 1)
                else:
                    c, before = (FS, L * B) if n == 0 else (S[PHASES[n - 1].name], (L + 1) * B)
                    dve.wait_ge(c["xstat"], before - (B - cols.stop))
                if stage == 0:
                    nc.vector.tensor_tensor(total, me, mo, ALU.add)
                    nc.vector.tensor_tensor(diff, me, mo, ALU.subtract)
                    ins = nc.vector.tensor_tensor(q, qe, qo, ALU.add)
                if stage == 1:
                    ins = nc.vector.tensor_tensor(diff, diff, diff, ALU.mult)
                if stage == 2:
                    ins = nc.vector.scalar_tensor_tensor(out=q, in0=diff, scalar=P / 4.0, in1=q, op0=ALU.mult, op1=ALU.add)
                if stage == 3:
                    ins = nc.vector.tensor_scalar(var, q, 1.0 / P, EPS, ALU.mult, ALU.add)
                if stage == 4:
                    ins = nc.vector.tensor_scalar(r.bitcast(I32), var.bitcast(I32), -0.5, float(RSQRT_BITS),
                                                  ALU.mult, ALU.add)
                if 5 <= stage < STAGES - 1:
                    if stage % 3 == 2:
                        ins = nc.vector.tensor_tensor(t, r, r, ALU.mult)
                    if stage % 3 == 0:
                        ins = nc.vector.scalar_tensor_tensor(out=t, in0=t, scalar=-0.5, in1=var, op0=ALU.mult, op1=ALU.mult)
                    if stage % 3 == 1:
                        ins = nc.vector.scalar_tensor_tensor(out=r, in0=t, scalar=1.5, in1=r, op0=ALU.add, op1=ALU.mult)
                if stage == STAGES - 1:
                    ins = nc.vector.scalar_tensor_tensor(out=nmr[:, cols], in0=total, scalar=-0.5, in1=r,
                                                         op0=ALU.mult, op1=ALU.mult)
                ins.then_inc(moments, 1)
                if stage == STAGES - 1:
                    dve.wait_ge(moments, base + STAGES)

            def row_norm(c, count, G, b, b0):
                if b == 0 and count is not None:
                    dve.wait_ge(c["xnT"], count)
                bb = b0 + b
                ins = nc.vector.tensor_scalar(xn[:, b, :], x[:, bb, :], rstd[:, bass.ds(bb, 1)],
                                              nmr[:, bass.ds(bb, 1)], ALU.mult, ALU.add)
                if b == G - 1:
                    ins.then_inc(c["xn"], 1)

            def rows_norm(c, count, G, b0):
                for b in range(G):
                    row_norm(c, count, G, b, b0)

            def rows_full(c, n, src, count, G):
                dve.wait_ge(c["xnT"], count)
                nc.vector.tensor_scalar(xfull[:, 0:G * P], src[:, 0:G * P],
                                        gb[:, n, 0:1], gb[:, n, 1:2], ALU.mult, ALU.add).then_inc(c["xfull"], 1)

            def rows_lo(c, count, G, par):
                dve.wait_ge(c["xhi"], count)
                nc.vector.tensor_tensor(xt_lo[:, par, 0:G * P], xfull[:, 0:G * P],
                                        xt_hi[:, par, 0:G * P].bitcast(F32), ALU.subtract).then_inc(c["xlo"], 1)

            def residual(c, n, src, y_count, bb, b, between=None):
                dve.wait_ge(c["y"], y_count)
                nc.vector.tensor_tensor(ytmp[:], src, bo_bc[:], ALU.add).then_inc(c["ysum"], 1)
                if between:
                    between(0)
                dve.wait_ge(c["ysum"], bb + 1)
                nc.vector.tensor_tensor(x[:, b, :], x[:, b, :], ytmp[:], ALU.add).then_inc(c["resid"], 1)
                if between:
                    between(1)
                dve.wait_ge(c["resid"], bb + 1)
                nc.vector.bn_stats(stats[:, b, :], x[:, b, :]).then_inc(c["xstat"], 1)

            def context_lo(n, ph, g, par):
                c = S[ph.name]
                if n == 1:
                    dve.wait_ge(c["chi"], g)
                    nc.vector.tensor_tensor(c_lo[:, par, :], craw[:].rearrange("p b j -> p (b j)"),
                                            c_hi[:, par, :].bitcast(F32), ALU.subtract).then_inc(c["clo"], 1)

            def item_lo(ph, it, base, wbase, off, v_free):
                kind, a, z, m, q = it
                c, J = S[ph.name], ph.J
                if kind == "w":
                    cols = slice(a * ph.HI * ph.GJ, (a + 1) * ph.HI * ph.GJ)
                    dve.wait_ge(c["whi"], wbase + (q + 1))
                    nc.vector.tensor_tensor(w_lo[:, z, cols], it_ps[(m + off) % IBANKS][:, 0:ph.HI * ph.GJ],
                                            w_hi[:, z, cols].bitcast(F32), ALU.subtract).then_inc(c["evac"], 1)
                else:
                    dve.wait_ge(c["item"], base + (m + 1))
                    if v_free is not None:
                        dve.wait_ge(c["pv"], v_free)
                    nc.vector.tensor_copy(v_sb[0:J, a % VRING, z * PS_BANK:(z + 1) * PS_BANK],
                                          it_ps[(m + off) % IBANKS][0:J, :]).then_inc(c["evac"], 1)

            def opening(L, n, part):
                c, G, groups = (S[PHASES[n].name], PHASES[n].G, L * PHASES[n].groups) if n < 2 else (FS, FG, L * (B // FG))
                if part == 0:
                    rows_norm(c, groups or None, G, 0)
                if part == 2:
                    if n == 2:
                        dve.wait_ge(f1_hi_s, L + 1)
                        nc.vector.tensor_tensor(f1_lo, raw_f, f1_hi.bitcast(F32), ALU.subtract).then_inc(f1_lo_s, 1)
                if part in (0, 2) and n < 2:
                    r, E = part // 2, PHASES[n].E
                    for odd in range(2):
                        heads = slice(8 * r + odd, 8 * r + 8, 2)
                        dve.wait_ge(wprod_hi, L * 8 + (4 * n + 2 * r + odd + 1))
                        nc.vector.scalar_tensor_tensor(out=a_lo[0:E, heads, :],
                                                       in0=it_ps[odd][0:E, :].rearrange("p (h n) -> p h n", h=4),
                                                       scalar=DH ** -0.5, in1=a_hi[0:E, heads, :].bitcast(F32),
                                                       op0=ALU.mult, op1=ALU.subtract).then_inc(wprod_lo, 1)
                if part == 1:
                    ln_ready(dve, L, n)
                    rows_full(c, n, it_ps[2], groups + 1, G)
                    rows_lo(c, groups + 1, G, 0)
                if n < 2:
                    ph, E = PHASES[n], PHASES[n].E
                    if part == 3:
                        dve.wait_ge(wv_hi_s, L * 2 + (n + 1))
                        nc.vector.tensor_tensor(wv_lo[0:E, :], raw_v[0:E, :], wv_hi[0:E, :].bitcast(F32),
                                                ALU.subtract).then_inc(wv_lo_s, 1)
                    if part == 4:
                        context_lo(n, ph, groups + 1, 0)
                    if part == OPEN_ITEMS:
                        dve.wait_ge(wv_lo_s, L * 2 + (n + 1))
                    for it in ph.prologue_part(part):
                        item_lo(ph, it, L * ph.items, L * (ph.w_per_group * ph.groups), 0, None)
                if part == OPEN_PARTS - 1:
                    rows_norm(c, groups + 1, G, G)
                    if n == 1:
                        context_lo(n, PHASES[n], groups + 2, 1)

            def attention(n, ph, L):
                c = S[ph.name]
                E, J, JP = ph.E, ph.J, ph.JP
                units, items, groups, batches = L * ph.units, L * ph.items, L * ph.groups, L * ph.B
                plans = {False: ph.body(False), True: ph.body(True)}

                def step(i, s, first, last_body):
                    k = units + (i * ph.UB + s)
                    its = []
                    if exists(ph.UB, s, first, last_body, 0):
                        g, gs = s // ph.U, s % ph.U
                        ib = items + (i * ph.items_per_body + ph.items_prologue)
                        wb = L * (ph.w_per_group * ph.groups) + (i * (2 * ph.w_per_group) + ph.w_per_group)
                        its = plans[last_body][s]

                        def v_free(it):
                            b = it[1]
                            if first and b < VRING:
                                return None
                            return units // 2 + (i * (ph.UB // 2) + (b - VRING + 1) * UPB // 2)
                        more = not (last_body and g == 1)
                        if gs == 0 and more:
                            rows_full(c, n, tr_ps, groups + (i * 2 + g + 2), ph.G)
                        dve.wait_ge(c["scores"], k + 1)
                        nc.vector.tensor_reduce(nmax[:, s % PRING, :],
                                                sc_ps[s % 2][:, 0:HG * JP].rearrange("p (h j) -> p h j", h=HG)[:, :, 0:J],
                                                AX.X, ALU.max, negate=True).then_inc(c["nmax"], 1)
                        for it in its[:1]:
                            item_lo(ph, it, ib, wb, ph.items_prologue, v_free(it))
                    if exists(ph.UB, s, first, last_body, EXP_LAG):
                        u = s - EXP_LAG
                        dve.wait_ge(c["exps"], k - EXP_LAG + 1)
                        nc.vector.reciprocal(rrec[:, u % PRING, :], rsum[:, u % PRING, :]).then_inc(c["recips"], 1)
                    if exists(ph.UB, s, first, last_body, PV_LAG) and (s - PV_LAG) % 2:
                        b, half = (s - PV_LAG) // UPB, (s - PV_LAG) % UPB // 2
                        dve.wait_ge(c["pv"], units // 2 + (i * (ph.UB // 2) + (s - PV_LAG) // 2 + 1))
                        if not (first and s - PV_LAG < UPB):
                            dve.wait_ge(c["y"], units // 2 + (i * (ph.UB // 2) + (s - PV_LAG) // 2 - 1))
                        nc.vector.tensor_copy(ot[:, half, :, :],
                                              ot_ps[:].rearrange("p (c n) -> p c n", n=P)).then_inc(c["ot"], 1)
                    for it in its[1:]:
                        item_lo(ph, it, ib, wb, ph.items_prologue, v_free(it))
                    if exists(ph.UB, s, first, last_body, Y_LAG) and (s - Y_LAG) % UPB == UPB - 1:
                        b = (s - Y_LAG) // UPB
                        bl = i * (2 * ph.G) + b
                        if first and b == 0:
                            par_ready(dve, L, n)
                        residual(c, n, y_ps[:, 0:P], batches * 2 + (bl * 2 + 2), batches + bl, bl)
                    if s < ph.UB and gs == 0 and more:
                        rows_lo(c, groups + (i * 2 + g + 2), ph.G, 1 - g)
                    if s < ph.UB and gs == ph.U - 2 and not last_body:
                        context_lo(n, ph, groups + (i * 2 + g + 3), g)
                        rows_norm(c, groups + (i * 2 + g + 2), ph.G, i * (2 * ph.G) + (g + 2) * ph.G)
                    start = (L, n) == (0, 0) and first
                    if start and s < STAT_STEPS:
                        rows_stats(X_PARTS[1] + s * STAT_ROWS, X_PARTS[1] + (s + 1) * STAT_ROWS)
                    stage0 = 2 * (s - STAT_STEPS if start else s)
                    for stage in range(max(stage0, 0), min(stage0 + 2, STAGES)):
                        if first:
                            statistics(L, n, 1, stage)
                        if last_body:
                            statistics(*following(L, n), 0, stage)
                    if last_body:
                        open_next(opening, L, n, s, ph)

                bodies(dve, ph.NI, ph.UB, Y_LAG, step)

            def feed_forward(L):
                c = FS
                groups, batches = L * (B // FG), L * B

                def stages(which, ch):
                    for j in range(2 * ch, min(2 * ch + 2, STAGES)):
                        statistics(*which, j)

                def step(i, s, first, last_body):
                    g = i * 2 + s
                    u = groups * FC + (i * (2 * FC) + s * FC)
                    here = exists(2, s, first, last_body, 0)
                    for ch in range(FC):
                        if here:
                            more = not (last_body and s == 1)
                            dve.wait_ge(c["a"], u + (ch + 1))
                            dve.wait_ge(c["gelu"], u + (ch + 1))
                            if ch == 0 and not (first and s < 2):
                                dve.wait_ge(c["y"], batches + (g - 1) * FG)
                            nc.vector.scalar_tensor_tensor(out=hid[:, s % 2, ch, :], in0=it_ps[ch % 2][:],
                                                           scalar=fb[:, ch:ch + 1], in1=gel[:, ch, :],
                                                           op0=ALU.add, op1=ALU.mult).then_inc(c["hid"], 1)
                            if ch == 1 and more:
                                rows_full(c, 2, y_ps, groups + (g + 2), FG)
                            if ch == 2 and more:
                                rows_lo(c, groups + (g + 2), FG, 1 - s)
                        if exists(2, s, first, last_body, 1):
                            bl = i * (2 * FG) + (s - 1) * FG + ch
                            if first and s == 1 and ch == 0:
                                par_ready(dve, L, 2)

                            def norm(half):
                                row_norm(c, groups + (g + 2), FG, 2 * (ch - 2) + half, i * (2 * FG) + (s + 2) * FG)
                            residual(c, 2, (ot_ps, tr_ps)[ch % 2][:, 0:P], batches + (bl + 1), batches + bl, bl,
                                     norm if ch >= 2 and not last_body else None)
                        elif ch == FC - 1 and not last_body:
                            rows_norm(c, groups + (g + 2), FG, i * (2 * FG) + (s + 2) * FG)
                        if first:
                            stages((L, 2, 1), s * FC + ch)
                        if last_body and s < 2 and following(L, 2):
                            stages((*following(L, 2), 0), s * FC + ch)
                        if s == 2:
                            open_next_ff(opening, L, ch)

                bodies(dve, FNI, 2, 1, step)

            rows_stats(0, X_PARTS[1])
            for stage in range(STAGES):
                statistics(0, 0, 0, stage)
            for part in range(OPEN_PARTS):
                opening(0, 0, part)
            for L in range(LAYERS):
                for n, ph in enumerate(PHASES):
                    attention(n, ph, L)
                feed_forward(L)


def kernel(**inputs):
    import numpy as np
    import concourse.bacc as bacc
    from concourse.bass_utils import run_bass_kernel_spmd as run

    def a(name):
        return np.asarray(inputs[name])

    L0, L1 = "L0_xattn_", "L1_xattn_"

    def both(f0, f1=None):
        return np.ascontiguousarray(np.stack([f0(L0), (f1 or f0)(L1)]))

    lay = {
        "x": np.ascontiguousarray(a("x")),
        "ctx_t": np.ascontiguousarray(a("ctx_768").transpose(2, 0, 1)),
        "wq_t": both(lambda p: np.stack([a(p + "Wq1").T, a(p + "Wq2").T])),
        "wk_t": both(lambda p: a(p + "Wk1").T),
        "wv": both(lambda p: a(p + "Wv1")),
        "wo": both(lambda p: np.stack([a(p + "Wo1"), a(p + "Wo2")])),
        "bo": both(lambda p: np.stack([a(p + "bo1"), a(p + "bo2"), a(p + "bff2")]),
                   lambda p: np.stack([a(p + "bo1"), a(p + "bo2"), a(p + "bf")])),
        "wk2_t": both(lambda p: a(p + "Wk2").T),
        "wv2": both(lambda p: a(p + "Wv2")),
        "ln_gb": both(lambda p: np.stack([np.stack([a(f"{p}ln{n}_g"), a(f"{p}ln{n}_b")], -1) for n in (1, 2, 3)]),
                     lambda p: np.stack([np.stack([a(f"{p}g{n}"), a(f"{p}b{n}")], -1) for n in (1, 2, 3)])),
        "w1": both(lambda p: a(p + "Wff1"), lambda p: a(p + "Wp")),
        "b1": both(lambda p: a(p + "bff1").reshape(-1, P).T, lambda p: a(p + "bp").reshape(-1, P).T),
        "w2": both(lambda p: a(p + "Wff2"), lambda p: a(p + "Wf")),
    }
    nc = bacc.Bacc("TRN2", target_bir_lowering=False, num_devices=1)
    aps = {k: nc.dram_tensor("in_" + k, v.shape, mybir.dt.from_np(v.dtype), kind="ExternalInput").ap() for k, v in lay.items()}
    y = nc.dram_tensor("out_y", lay["x"].shape, F32, kind="ExternalOutput").ap()
    block_kernel(nc, aps["x"], aps["ctx_t"], aps["wq_t"], aps["wk_t"], aps["wv"], aps["wo"], aps["bo"],
                 aps["wk2_t"], aps["wv2"], aps["ln_gb"], aps["w1"], aps["b1"], aps["w2"], y)
    r = run(nc, [{"in_" + k: v for k, v in lay.items()}], core_ids=[0])
    return r.results[0]["out_y"]
```
